# Optimizing a Trainium2 kernel written in Bass

```python
import numpy as np
import jax
import jax.numpy as jnp

def _softmax(x, axis=-1):
    return jax.nn.softmax(x, axis=axis)

def _gelu(x):
    return jax.nn.gelu(x, approximate=True)

def _silu(x):
    return jax.nn.silu(x)

def _sigmoid(x):
    return jax.nn.sigmoid(x)

def _layernorm(x, axis=-1, eps=1e-05):
    m = jnp.mean(x, axis=axis, keepdims=True)
    v = jnp.var(x, axis=axis, keepdims=True)
    return (x - m) / jnp.sqrt(v + eps)

def _scatter_add(tgt, idx, src, axis=0):
    return tgt.at[idx].add(src)

def _segment_sum(src, seg, n):
    return jax.ops.segment_sum(src, seg, n)
kernel_name = 'mk_flamingo_gated_d1_seqx_r8_45d129'

def setup_inputs(seed: int=0):
    np.random.seed(seed)
    _w = jnp.asarray

    def _rec_inputs():
        import jax
        import jax.numpy as jnp
        _rk = jax.random.key(seed)
        x = -0.0002928 + 1 * jax.random.normal(jax.random.fold_in(_rk, 1), (2, 256, 256), jnp.float32)
        _lenS = 256 - jax.random.randint(jax.random.fold_in(_rk, 7), (2,), 0, max(1, 256 // 4) + 1, jnp.int32)
        _lenS2 = 512 - jax.random.randint(jax.random.fold_in(_rk, 8), (2,), 0, max(1, 512 // 4) + 1, jnp.int32)
        _ctx_512P = jax.random.normal(jax.random.fold_in(_rk, 11), (2, 16, 64), jnp.float32)
        _ctx_512c = jax.random.dirichlet(jax.random.fold_in(_rk, 511), 0.3 * jnp.ones((16,), jnp.float32), (2, 512))
        _ctx_512t = jnp.einsum('bsk,bkd->bsd', _ctx_512c, _ctx_512P)
        _ctx_512t = _ctx_512t * jax.lax.rsqrt(jnp.mean(jnp.square(_ctx_512t)) + 1e-12) * 0.953939
        ctx_512 = 0.000227908 + 0.99994 * (_ctx_512t + 0.3 * jax.random.normal(jax.random.fold_in(_rk, 611), (2, 512, 64), jnp.float32))
        _g = jax.random.normal(jax.random.fold_in(_rk, 9001), (2, 1), jnp.float32)
        _g = jnp.sign(_g) * jnp.maximum(jnp.abs(_g), 1.0) + (_g == 0) * 1.0
        g_xattn = _g[0]
        g_ffn = _g[1]
        return (x, ctx_512, g_xattn, g_ffn)
    x, ctx_512, g_xattn, g_ffn = _rec_inputs()

    def _L0_xattn_setup():
        import jax, jax.numpy as jnp
        import numpy as np
        B, S, L = (2, 128, 128)
        DIM_Q, H, K, D_C, D_CQ, R = (256, 16, 128, 64, 192, 64)

        def _rope_tables(seq_len, dim, dtype):
            inv_freq = 1.0 / 10000.0 ** (jnp.arange(0, dim, 2, dtype=dtype) / dim)
            t = jnp.arange(seq_len, dtype=dtype)
            freqs = t[:, None] * inv_freq[None, :]
            sin = jnp.repeat(jnp.sin(freqs), 2, axis=-1)
            cos = jnp.repeat(jnp.cos(freqs), 2, axis=-1)
            return (sin, cos)

        def _rotate_half(x):
            h = x.shape[-1] // 2
            return jnp.concatenate([-x[..., h:], x[..., :h]], axis=-1)
        key = jax.random.key(seed)
        ks = jax.random.split(key, 8)
        s_in = 1.0 / np.sqrt(DIM_Q)
        s_k = 1.0 / np.sqrt(K)
        s_cq = 1.0 / np.sqrt(D_CQ)
        s_c = 1.0 / np.sqrt(D_C)
        return {'hidden_q': jax.random.normal(ks[0], (B, S, DIM_Q), jnp.float32), 'kv_c': jax.random.normal(ks[1], (B, L, D_C), jnp.float32), 'Wq': jax.random.normal(ks[2], (H * K, DIM_Q), jnp.float32) * s_in, 'w_kc_q': jax.random.normal(ks[3], (H, K, D_CQ), jnp.float32) * s_k, 'w_kc_kv': jax.random.normal(ks[4], (H, K, D_C), jnp.float32) * s_k, 'W_qr': jax.random.normal(ks[5], (H, D_CQ, R), jnp.float32) * s_cq / np.sqrt(R), 'W_kr': jax.random.normal(ks[6], (H, D_C, R), jnp.float32) * s_c, 'Wo': jax.random.normal(ks[7], (DIM_Q, H * K), jnp.float32) * s_k}
    _L0_xattn_all = _L0_xattn_setup()
    _L0_xattn_in = {k: v for k, v in _L0_xattn_all.items() if k in ('Wq', 'w_kc_q', 'w_kc_kv', 'W_qr', 'W_kr', 'Wo')}
    del _L0_xattn_all

    def _L0_ffn_setup():
        import jax, jax.numpy as jnp
        import numpy as np
        H = 256
        E = 64
        I = 64
        SI = 64
        TOP_K = 8
        B, T = (2, 64)
        key = jax.random.key(seed)
        ks = jax.random.split(key, 8)
        s = 0.02
        return {'h': jax.random.normal(ks[0], (B, T, H), jnp.float32), 'gate_w': jax.random.normal(ks[1], (E, H), jnp.float32) * s, 'gu_w': jax.random.normal(ks[2], (E, 2 * I, H), jnp.float32) * s, 'dp_w': jax.random.normal(ks[3], (E, H, I), jnp.float32) * s, 'sh_gate_w': jax.random.normal(ks[4], (SI, H), jnp.float32) * s, 'sh_up_w': jax.random.normal(ks[5], (SI, H), jnp.float32) * s, 'sh_down_w': jax.random.normal(ks[6], (H, SI), jnp.float32) * s, 'sh_gate1_w': jax.random.normal(ks[7], (1, H), jnp.float32) * s}
    _L0_ffn_all = _L0_ffn_setup()
    _L0_ffn_in = {k: v for k, v in _L0_ffn_all.items() if k in ('gate_w', 'gu_w', 'dp_w', 'sh_gate_w', 'sh_up_w', 'sh_down_w', 'sh_gate1_w')}
    del _L0_ffn_all
    return {'x': x, 'ctx_512': ctx_512, 'g_xattn': g_xattn, 'g_ffn': g_ffn, 'L0_xattn_Wq': _L0_xattn_in['Wq'], 'L0_xattn_w_kc_q': _L0_xattn_in['w_kc_q'], 'L0_xattn_w_kc_kv': _L0_xattn_in['w_kc_kv'], 'L0_xattn_W_qr': _L0_xattn_in['W_qr'], 'L0_xattn_W_kr': _L0_xattn_in['W_kr'], 'L0_xattn_Wo': _L0_xattn_in['Wo'], 'L0_ffn_gate_w': _L0_ffn_in['gate_w'], 'L0_ffn_gu_w': _L0_ffn_in['gu_w'], 'L0_ffn_dp_w': _L0_ffn_in['dp_w'], 'L0_ffn_sh_gate_w': _L0_ffn_in['sh_gate_w'], 'L0_ffn_sh_up_w': _L0_ffn_in['sh_up_w'], 'L0_ffn_sh_down_w': _L0_ffn_in['sh_down_w'], 'L0_ffn_sh_gate1_w': _L0_ffn_in['sh_gate1_w']}

def reference(x, ctx_512, g_xattn, g_ffn, L0_xattn_Wq, L0_xattn_w_kc_q, L0_xattn_w_kc_kv, L0_xattn_W_qr, L0_xattn_W_kr, L0_xattn_Wo, L0_ffn_gate_w, L0_ffn_gu_w, L0_ffn_dp_w, L0_ffn_sh_gate_w, L0_ffn_sh_up_w, L0_ffn_sh_down_w, L0_ffn_sh_gate1_w):
    import jax
    import jax.numpy as jnp

    def _L0_xattn_ref(hidden_q, kv_c, Wq, w_kc_q, w_kc_kv, W_qr, W_kr, Wo):
        import jax, jax.numpy as jnp
        import numpy as np
        B, S, L = (2, 128, 128)
        DIM_Q, H, K, D_C, D_CQ, R = (256, 16, 128, 64, 192, 64)

        def _rope_tables(seq_len, dim, dtype):
            inv_freq = 1.0 / 10000.0 ** (jnp.arange(0, dim, 2, dtype=dtype) / dim)
            t = jnp.arange(seq_len, dtype=dtype)
            freqs = t[:, None] * inv_freq[None, :]
            sin = jnp.repeat(jnp.sin(freqs), 2, axis=-1)
            cos = jnp.repeat(jnp.cos(freqs), 2, axis=-1)
            return (sin, cos)

        def _rotate_half(x):
            h = x.shape[-1] // 2
            return jnp.concatenate([-x[..., h:], x[..., :h]], axis=-1)
        b, s, _ = hidden_q.shape
        l = kv_c.shape[1]
        q_hk = (hidden_q @ Wq.T).reshape(b, s, H, K)
        q_big = jnp.einsum('bshk,hkq->bshq', q_hk, w_kc_q)
        sin, cos = _rope_tables(l, D_C, kv_c.dtype)
        kv_rope = kv_c * cos[None] + _rotate_half(kv_c) * sin[None]
        q_r = jnp.einsum('bshq,hqr->bhsr', q_big, W_qr)
        k_r = jnp.einsum('bld,hdr->bhlr', kv_rope, W_kr)
        scores = jnp.einsum('bhsr,bhlr->bhsl', q_r, k_r)
        attn = jax.nn.softmax(scores, axis=-1)
        ctx_c = jnp.einsum('bhsl,bld->bhsd', attn, kv_rope)
        ctx_lat = jnp.einsum('bhsd,hkd->bshk', ctx_c, w_kc_kv)
        out = ctx_lat.reshape(b, s, H * K) @ Wo.T
        return out

    def _L0_ffn_ref(h, gate_w, gu_w, dp_w, sh_gate_w, sh_up_w, sh_down_w, sh_gate1_w):
        import jax, jax.numpy as jnp
        import numpy as np
        H = 256
        E = 64
        I = 64
        SI = 64
        TOP_K = 8
        B, T = (2, 64)
        Bb, Tt, Hh = h.shape
        x = h.reshape(Bb * Tt, Hh)
        N = x.shape[0]
        logits = x @ gate_w.T
        topv, topi = jax.lax.top_k(logits, TOP_K)
        rw = jax.nn.softmax(topv.astype(jnp.float32), axis=-1).astype(x.dtype)
        W = jnp.zeros((N, E), x.dtype).at[jnp.arange(N)[:, None], topi].set(rw)
        gu = jnp.einsum('nh,eih->nei', x, gu_w)
        gate, up = (gu[..., :I], gu[..., I:])
        inter = jax.nn.silu(gate) * up
        inter_w = inter * W[:, :, None]
        out = jnp.einsum('nei,ehi->nh', inter_w, dp_w)
        sh_inter = jax.nn.silu(x @ sh_gate_w.T) * (x @ sh_up_w.T)
        sh_out = sh_inter @ sh_down_w.T
        sh_g = jax.nn.sigmoid(x @ sh_gate1_w.T)
        out = out + sh_g * sh_out
        return out.reshape(Bb, Tt, Hh)
    x = x + jnp.tanh(g_xattn[0]) * _L0_xattn_ref(_layernorm(x, axis=-1), ctx_512, L0_xattn_Wq, L0_xattn_w_kc_q, L0_xattn_w_kc_kv, L0_xattn_W_qr, L0_xattn_W_kr, L0_xattn_Wo)
    x = x + jnp.tanh(g_ffn[0]) * _L0_ffn_ref(_layernorm(x, axis=-1), L0_ffn_gate_w, L0_ffn_gu_w, L0_ffn_dp_w, L0_ffn_sh_gate_w, L0_ffn_sh_up_w, L0_ffn_sh_down_w, L0_ffn_sh_gate1_w)
    return x

_drawn_inputs = setup_inputs


def setup_inputs(seed=0):
    import zlib

    import numpy as np

    out = dict(_drawn_inputs(seed))
    spreads = {}
    factors = {'L0_ffn_gate_w': 8.0,
     'L0_ffn_gu_w': 8.0,
     'L0_ffn_dp_w': 8.0,
     'L0_ffn_sh_gate_w': 8.0,
     'L0_ffn_sh_up_w': 8.0,
     'L0_ffn_sh_down_w': 8.0,
     'L0_ffn_sh_gate1_w': 8.0}
    for name, (base, spread) in spreads.items():
        noise = np.random.default_rng([zlib.crc32(name.encode()), seed]).standard_normal(out[name].shape)
        drawn = base * np.exp(spread * noise) if base else spread * noise
        out[name] = jnp.asarray(drawn.astype(out[name].dtype))
    for name, factor in factors.items():
        out[name] = (out[name] * factor).astype(out[name].dtype)
    return out
```

```python
from contextlib import ExitStack

import concourse.bass as bass
from concourse import mybir
from concourse.alu_op_type import AluOpType as ALU

F32 = mybir.dt.float32
F32R = mybir.dt.float32r
ACT = mybir.ActivationFunctionType
AX = mybir.AxisListType.X

P = 128
B, S, DIM = 2, 256, 256
L, DC = 512, 64
H, HK, CQ, R = 16, 128, 192, 64
E, EI, TOPK = 64, 64, 8
LN_EPS = 1e-5

TOK = B * S
NT = TOK // P
NC = DIM // P
NS = S // P
NL = L // P
HP = H // 2
QH = CQ // 2
TILES = B * 2 * NS
EP = E // 2
NP = EP + 1
PER_HEAD = DIM + DC + DIM
W1COLS = 2 * 2 * (R + HK)
W2COLS = DC + 2 * PER_HEAD
GU = NC * 2 * P
FW = GU + DIM
RING = 4
CI, CC, CS, CZ = 0, P, P + NL * DC, P + 2 * NL * DC
CONSTS = CZ + E


def gated_cross_attention_moe(nc, x, ctx, consts, gains, w_fold_q, w_fold_kv, gate_w, shared_gate1, w_experts, out):
    with ExitStack() as stack:
        def sb(name, shape, dt=F32):
            return stack.enter_context(nc.sbuf_tensor(name, shape, dt))

        def sem(name):
            return stack.enter_context(nc.semaphore(name))

        bank = [stack.enter_context(nc.psum_tensor(f"bank{i}", [P, 512], F32)) for i in range(8)]

        x_sb = sb("x_sb", [P, NT, DIM])
        ctx_sb = sb("ctx_sb", [P, B, NL, DC])
        con = sb("con", [P, CONSTS])
        gain_raw = sb("gain_raw", [P, 2])
        gain = sb("gain", [P, 2])
        eps = sb("eps", [P, 1])
        gate_raw = sb("gate_raw", [P, NC, E])
        gate_hl = sb("gate_hl", [P, NC, 2, E], F32R)
        g1_raw = sb("g1_raw", [P, NC, P])
        g1_hi = sb("g1_hi", [P, NC, P], F32R)
        g1_lo = sb("g1_lo", [P, NC, P], F32R)

        stats = sb("stats", [P, NT, 6])
        meanvar = sb("meanvar", [P, NT, 2])
        stdev = sb("stdev", [P, NT])
        rstd = sb("rstd", [P, NT])
        normed = sb("normed", [P, NT, DIM])
        nT_hi = sb("nT_hi", [P, NC, TOK], F32R)
        nT_lo = sb("nT_lo", [P, NC, TOK], F32R)

        kv = sb("kv", [P, B * NL, 2, DC])
        rot = sb("rot", [P, B * NL, DC])
        K_hi = sb("K_hi", [P, B, L], F32R)
        K_lo = sb("K_lo", [P, B, L], F32R)

        raw_q = sb("raw_q", [QH, W1COLS])
        raw_kv = sb("raw_kv", [P, W2COLS])
        rT = sb("rT", [P, HK])
        foldF = sb("foldF", [P, 2, DC])
        A_hi = sb("A_hi", [P, NC, P], F32R)
        A_lo = sb("A_lo", [P, NC, P], F32R)
        Bout = sb("Bout", [P, HP, DIM])
        Q = [sb(f"Q{h}", [P, TOK], F32R) for h in range(2)]
        nmax = sb("nmax", [P, TILES])
        rsum = sb("rsum", [P, TILES])
        rinv = sb("rinv", [P, TILES])
        prob = [sb(f"prob{i}", [P, L]) for i in range(4)]
        probT = [[sb(f"probT{b}{h}", [P, NL, S]) for h in range(2)] for b in range(B)]
        ctxT = sb("ctxT", [P, HP, TOK])

        x1 = sb("x1", [P, NT, DIM])
        logit = sb("logit", [P, NT, E])
        top8 = sb("top8", [P, NT, TOPK])
        cut = sb("cut", [P, NT, E])
        shifted = sb("shifted", [P, NT, E])
        chosen = sb("chosen", [P, NT, E])
        expl = sb("expl", [P, NT, E])
        picked = sb("picked", [P, NT, E])
        psumw = sb("psumw", [P, NT])
        pinv = sb("pinv", [P, NT])
        route = sb("route", [P, NT, E])
        routeT = sb("routeT", [P, TOK], F32R)

        ffn_raw = [sb(f"ffn_raw{i}", [P, FW]) for i in range(RING)]
        ffn_hi = [sb(f"ffn_hi{i}", [P, FW], F32R) for i in range(RING)]
        ffn_lo = [sb(f"ffn_lo{i}", [P, FW], F32R) for i in range(RING)]
        pick = [sb(f"pick{i}", [P, P], F32R) for i in range(RING)]
        act_g = [sb(f"act_g{i}", [P, TOK]) for i in range(2)]
        shared_g = sb("shared_g", [P, TOK])
        gu = [sb(f"gu{i}", [P, TOK]) for i in range(2)]
        weighted = [sb(f"weighted{i}", [P, TOK]) for i in range(2)]
        in_hi = [sb(f"in_hi{i}", [P, TOK], F32R) for i in range(2)]
        in_lo = [sb(f"in_lo{i}", [P, TOK], F32R) for i in range(2)]
        outT = sb("outT", [P, NC, TOK])
        fin = sb("fin", [P, NT, DIM])

        ident = con[:, CI:CI + P]
        cos = con[:, CC:CC + NL * DC].rearrange("p (l d) -> p l d", l=NL)
        sin = con[:, CS:CS + NL * DC].rearrange("p (l d) -> p l d", l=NL)
        stacked = con[:, CZ:CZ + E]

        names = """x_loaded ctx_loaded con_loaded fold_loaded small_loaded out_stored
            eps_set stat1 mv1 sd1 rstd1 norm1 xT1 xhi1 xlo1
            rope_cos rope_sin rope_done kT_made k_hi k_lo
            rT_made rT_copied F_made F_copied A_made A_hi_made A_lo_made B_made B_copied
            q_made q_hi q_lo scored max_made exp_made inv_made normalised transposed probT_copied
            attended ctx_copied gain_made gain_done
            out_made x1_made stat2 mv2 sd2 rstd2 norm2 xT2 xhi2 xlo2
            gate_hi gate_lo g1_split g1_rest logits_made logits_copied top_made cut_made shift_made chosen_made expl_made
            picked_made sum_made pinv_made route_made routeT_made routeT_hi routeT_lo
            w_hi w_lo pick_made gate_mm up_mm weight_mm silu_made shared_g_made gu_made weighted_made in_hi_made
            in_ready down_mm outT_copied outT_t fin_made""".split()
        s = {n: sem(n) for n in names}
        ffn_loaded = [sem(f"ffn_loaded{i}") for i in range(RING)]

        block = stack.enter_context(nc.Block())

        wq_r = w_fold_q.rearrange("t p n -> p t n")
        wkv_r = w_fold_kv.rearrange("t p n -> p t n")
        wf_r = w_experts.rearrange("t p n -> p t n")

        def tile_of(i):
            return i // (2 * NS), i // NS % 2, i % NS

        def dyn(ap3, t):
            return ap3[:, bass.ds(t, 1), :].rearrange("p a n -> p (a n)")

        @block.sync
        def _(sp):
            sp.dma_start(x_sb[:, :, :], x).then_inc(s["x_loaded"], 16)
            sp.dma_start(con[:, :], consts).then_inc(s["con_loaded"], 16)

            def load_fold(t):
                sp.dma_start(raw_q[:, :], dyn(wq_r, t)).then_inc(s["fold_loaded"], 16)
                sp.dma_start(raw_kv[:, :], dyn(wkv_r, t)).then_inc(s["fold_loaded"], 16)

            load_fold(0)
            sp.dma_start(ctx_sb[:, :, :, :], ctx).then_inc(s["ctx_loaded"], 16)
            sp.dma_start(gain_raw[:, :], gains).then_inc(s["small_loaded"], 16)
            sp.dma_start(gate_raw[:, :, :], gate_w).then_inc(s["small_loaded"], 16)
            sp.dma_start(g1_raw[:, :, :], shared_gate1).then_inc(s["small_loaded"], 16)
            for q in range(RING):
                sp.dma_start(ffn_raw[q][:, :], dyn(wf_r, q)).then_inc(ffn_loaded[q], 16)
            with sp.Fori(1, HP) as t:
                sp.wait_ge(s["B_made"], t)
                load_fold(t)
            with sp.Fori(0, (NP - 1 - RING) // RING) as u:
                for j in range(RING):
                    sp.wait_ge(s["w_lo"], u * RING + j + 1)
                    sp.dma_start(ffn_raw[j][:, :], dyn(wf_r, u * RING + j + RING)).then_inc(ffn_loaded[j], 16)
            for q in range(NP - 1 - (NP - 1) % RING, NP):
                sp.wait_ge(s["w_lo"], q - RING + 1)
                sp.dma_start(ffn_raw[q % RING][:, :], wf_r[:, q, :]).then_inc(ffn_loaded[q % RING], 16)
            for tt in range(NT):
                sp.wait_ge(s["fin_made"], tt + 1)
                sp.dma_start(out[:, tt, :], fin[:, tt, :]).then_inc(s["out_stored"], 16)
            sp.wait_ge(s["out_stored"], 16 * NT)

        @block.gpsimd
        def _(pool):
            def split_lo(slot, q):
                pool.wait_ge(s["w_hi"], q + 1)
                nc.gpsimd.tensor_tensor(ffn_lo[slot][:, :], ffn_raw[slot][:, :], ffn_hi[slot][:, :].bitcast(F32),
                                        ALU.subtract).then_inc(s["w_lo"], 1)

            pool.wait_ge(s["small_loaded"], 48)
            pool.wait_ge(s["gate_hi"], 1)
            nc.gpsimd.tensor_tensor(gate_hl[:, :, 1, :], gate_raw[:, :, :], gate_hl[:, :, 0, :].bitcast(F32),
                                    ALU.subtract).then_inc(s["gate_lo"], 1)
            pool.wait_ge(s["g1_split"], 1)
            nc.gpsimd.tensor_tensor(g1_lo[:, :, :], g1_raw[:, :, :], g1_hi[:, :, :].bitcast(F32),
                                    ALU.subtract).then_inc(s["g1_rest"], 1)
            for q in range(2):
                split_lo(q, q)
            with pool.Fori(0, (NP - 1) // RING - 1) as u:
                for j in range(RING):
                    split_lo((2 + j) % RING, u * RING + j + 2)
            for q in range(NP - 1 - RING + 2, NP):
                split_lo(q % RING, q)

        @block.scalar
        def _(act):
            def copy(dst, src, done):
                nc.scalar.activation(dst, src, ACT.Copy).then_inc(s[done], 1)

            act.wait_ge(s["mv1"], NT)
            nc.scalar.activation(stdev[:, :], meanvar[:, :, 1], ACT.Sqrt, bias=eps[:, 0:1]).then_inc(s["sd1"], 1)
            act.preload_act_table(ACT.Exp)

            def fold_hi(t):
                act.wait_ge(s["A_made"], t + 1)
                copy(A_hi[:, :, :], bank[6][:, 0:NC * P].rearrange("p (c n) -> p c n", c=NC), "A_hi_made")

            def split_nT_hi(tt, b, made, done):
                act.wait_ge(s[made], tt + 1)
                copy(nT_hi[:, :, tt * P:(tt + 1) * P], bank[b][:, 0:NC * P].rearrange("p (c n) -> p c n", c=NC), done)

            for b in range(B):
                act.wait_ge(s["kT_made"], b + 1)
                copy(K_hi[:, b, :], bank[b][:, :], "k_hi")
            for tt in range(NT):
                split_nT_hi(tt, 2 + tt % 2, "xT1", "xhi1")
            fold_hi(0)

            def q_hi(t, h):
                act.wait_ge(s["q_made"], t + 1)
                copy(Q[h][0:DC, :], bank[5][DC * h:DC * h + DC, :], "q_hi")

            for h in range(2):
                q_hi(0, h)
            act.wait_ge(s["small_loaded"], 48)
            copy(gate_hl[:, :, 0, :], gate_raw[:, :, :], "gate_hi")
            copy(g1_hi[:, :, :], g1_raw[:, :, :], "g1_split")
            nc.scalar.activation(gain[:, :], gain_raw[:, :], ACT.Tanh).then_inc(s["gain_done"], 1)

            def exponentials(t, i):
                act.wait_ge(s["max_made"], t * TILES + i + 1)
                nc.scalar.activation(prob[i % 4][:, :], bank[i % 2][:, :], ACT.Exp, bias=nmax[:, i:i + 1],
                                     accum_out=rsum[:, i:i + 1]).then_inc(s["exp_made"], 1)

            def copy_probT(t, i):
                b, h, sc = tile_of(i)
                act.wait_ge(s["transposed"], t * TILES + i + 1)
                copy(probT[b][h][:, :, sc * P:(sc + 1) * P], bank[2 + i % 2][:, :].rearrange("p (l n) -> p l n", l=NL),
                     "probT_copied")

            def pair(t, last):
                for i in range(TILES):
                    exponentials(t, i)
                    if i >= 2:
                        copy_probT(t, i - 2)
                    if i == 4 and not last:
                        fold_hi(t + 1)
                copy_probT(t, TILES - 2)
                if not last:
                    q_hi(t + 1, 0)
                copy_probT(t, TILES - 1)
                if not last:
                    q_hi(t + 1, 1)

            with act.Fori(0, HP - 1) as t:
                pair(t, False)
            pair(HP - 1, True)

            def weights_hi(slot, q):
                act.wait_ge(ffn_loaded[slot], (q // RING) * 16 + 16)
                copy(ffn_hi[slot][:, :], ffn_raw[slot][:, :], "w_hi")

            weights_hi(0, 0)
            weights_hi(1, 1)
            for tt in range(NT):
                act.wait_ge(s["mv2"], tt + 1)
                nc.scalar.activation(stdev[:, tt:tt + 1], meanvar[:, tt, 1:2], ACT.Sqrt,
                                     bias=eps[:, 0:1]).then_inc(s["sd2"], 1)
                if tt:
                    split_nT_hi(tt - 1, 4 + (tt - 1) % 2, "xT2", "xhi2")
            act.preload_act_table(ACT.Exp)
            split_nT_hi(NT - 1, 4 + (NT - 1) % 2, "xT2", "xhi2")
            act.wait_ge(s["shift_made"], 1)
            nc.scalar.activation(expl[:, :, :], shifted[:, :, :], ACT.Exp).then_inc(s["expl_made"], 1)
            act.wait_ge(s["weight_mm"], 1)
            nc.scalar.activation(shared_g[:, :], bank[4][:, :], ACT.Sigmoid).then_inc(s["shared_g_made"], 1)
            act.preload_act_table(ACT.Silu)

            def silu(j, q, first=False):
                act.wait_ge(s["gate_mm"], q + 1)
                if not first:
                    act.wait_ge(s["gu_made"], q - 1)
                nc.scalar.activation(act_g[j % 2][:, :], bank[j % 2][:, :], ACT.Silu).then_inc(s["silu_made"], 1)

            def make_pick(slot, q):
                src = stacked[:, bass.ds((q - 1) * 2, 2)]
                nc.scalar.activation(pick[slot][:, :].rearrange("p (e n) -> p e n", e=2),
                                     src.unsqueeze(2).to_broadcast([P, 2, EI]), ACT.Copy).then_inc(s["pick_made"], 1)

            def ffn_pair(j, q):
                silu(j, q)

            silu(0, 0, first=True)
            act.wait_ge(s["routeT_made"], 1)
            copy(routeT[0:E, :], bank[3][0:E, :], "routeT_hi")
            make_pick(1, 1)
            make_pick(2, 2)
            weights_hi(2, 2)

            def step(j, q, ahead=True):
                silu(j, q)
                if ahead:
                    act.wait_ge(s["down_mm"], q - 1)
                    slot = (j + 2) % RING
                    act.wait_ge(ffn_loaded[slot], ((j + 2) // RING) * 16 + (q - j) * (16 // RING) + 16)
                    copy(ffn_hi[slot][:, :], ffn_raw[slot][:, :], "w_hi")
                    make_pick(slot, q + 2)

            silu(1, 1, first=True)
            act.wait_ge(ffn_loaded[3], 16)
            copy(ffn_hi[3][:, :], ffn_raw[3][:, :], "w_hi")
            make_pick(3, 3)
            for j in range(2, RING):
                step(j, j)
            step(RING, RING)
            with act.Fori(1, (NP - 1) // RING - 1) as u:
                for j in range(1, RING + 1):
                    step(j, u * RING + j)
            for q in range(NP - RING, NP):
                step((q - 1) % RING + 1 if False else q, q, ahead=q + 2 < NP)

            for c in range(NC):
                act.wait_ge(s["down_mm"], NP)
                if c == 0:
                    copy(outT[:, c, :], bank[6 + c][:, :], "outT_copied")

        @block.vector
        def _(dve):
            v = nc.vector

            def hold(name, n):
                dve.wait_ge(s[name], n)

            v.memset(eps[:, :], LN_EPS).then_inc(s["eps_set"], 1)
            hold("x_loaded", 16)
            for tt in range(NT):
                v.bn_stats(stats[:, tt, :], x_sb[:, tt, :]).then_inc(s["stat1"], 1)
            for tt in range(NT):
                hold("stat1", tt + 1)
                v.bn_aggr(meanvar[:, tt, :], stats[:, tt, :]).then_inc(s["mv1"], 1)
            hold("sd1", 1)
            v.reciprocal(rstd[:, :], stdev[:, :]).then_inc(s["rstd1"], 1)
            hold("rstd1", 1)
            for tt in range(NT):
                v.tensor_scalar(normed[:, tt, :], x_sb[:, tt, :], meanvar[:, tt, 0:1], rstd[:, tt:tt + 1],
                                ALU.subtract, ALU.mult).then_inc(s["norm1"], 1)
            hold("con_loaded", 16)
            hold("ctx_loaded", 16)
            half = DC // 2
            for b in range(B):
                rows = slice(b * NL, (b + 1) * NL)
                v.tensor_tensor(rot[:, rows, 0:half], ctx_sb[:, b, :, half:DC], sin[:, :, 0:half],
                                ALU.mult).then_inc(s["rope_sin"], 1)
                v.tensor_tensor(rot[:, rows, half:DC], ctx_sb[:, b, :, 0:half], sin[:, :, half:DC],
                                ALU.mult).then_inc(s["rope_sin"], 1)
                v.tensor_tensor(kv[:, rows, 0, :], ctx_sb[:, b, :, :], cos, ALU.mult).then_inc(s["rope_cos"], 1)
            for b in range(B):
                rows = slice(b * NL, (b + 1) * NL)
                hold("rope_sin", 2 * b + 2)
                hold("rope_cos", b + 1)
                v.tensor_tensor(kv[:, rows, 1, :], kv[:, rows, 0, :], rot[:, rows, :], ALU.add)
                v.tensor_tensor(kv[:, rows, 0, :], kv[:, rows, 0, :], rot[:, rows, :],
                                ALU.add).then_inc(s["rope_done"], 1)

            def copy_rT(t):
                hold("rT_made", t + 1)
                v.tensor_copy(rT[:, :], bank[6][:, 0:HK]).then_inc(s["rT_copied"], 1)

            def copy_F(t):
                hold("F_made", t + 1)
                v.tensor_copy(foldF[:, 0, :], bank[6][:, 0:DC]).then_inc(s["F_copied"], 1)
                v.tensor_copy(foldF[:, 1, :], bank[7][:, 0:DC]).then_inc(s["F_copied"], 1)

            def copy_B(t):
                hold("B_made", t + 1)
                v.tensor_copy(dyn(Bout, t), bank[7][:, 0:DIM]).then_inc(s["B_copied"], 1)

            def fold_lo(t):
                hold("A_hi_made", t + 1)
                v.tensor_tensor(A_lo[:, :, :], bank[6][:, 0:NC * P].rearrange("p (c n) -> p c n", c=NC),
                                A_hi[:, :, :].bitcast(F32), ALU.subtract).then_inc(s["A_lo_made"], 1)

            def q_lo(t, h):
                hold("q_hi", 2 * t + h + 1)
                v.tensor_tensor(Q[h][DC:P, :], bank[5][DC * h:DC * h + DC, :], Q[h][0:DC, :].bitcast(F32),
                                ALU.subtract).then_inc(s["q_lo"], 1)

            def split_nT_lo(tt, b, hi, done):
                hold(hi, tt + 1)
                v.tensor_tensor(nT_lo[:, :, tt * P:(tt + 1) * P],
                                bank[b][:, 0:NC * P].rearrange("p (c n) -> p c n", c=NC),
                                nT_hi[:, :, tt * P:(tt + 1) * P].bitcast(F32), ALU.subtract).then_inc(s[done], 1)

            copy_rT(0)
            copy_F(0)
            for b in range(B):
                hold("k_hi", b + 1)
                v.tensor_tensor(K_lo[:, b, :], bank[b][:, :], K_hi[:, b, :].bitcast(F32),
                                ALU.subtract).then_inc(s["k_lo"], 1)
            for tt in range(NT):
                split_nT_lo(tt, 2 + tt % 2, "xhi1", "xlo1")
            copy_B(0)
            fold_lo(0)
            for h in range(2):
                q_lo(0, h)

            def row_max(t, i):
                hold("scored", t * TILES + i + 1)
                v.tensor_reduce(nmax[:, i:i + 1], bank[i % 2][:, :], AX, ALU.max, negate=True).then_inc(s["max_made"], 1)

            def invert(t, i):
                hold("exp_made", t * TILES + i + 1)
                v.reciprocal(rinv[:, i:i + 1], rsum[:, i:i + 1]).then_inc(s["inv_made"], 1)

            def normalise(t, i):
                hold("inv_made", t * TILES + i + 1)
                v.tensor_scalar(prob[i % 4][:, :], prob[i % 4][:, :], rinv[:, i:i + 1], None,
                                ALU.mult).then_inc(s["normalised"], 1)

            def copy_ctx(t, b):
                hold("attended", t * B + b + 1)
                v.tensor_copy(dyn(ctxT[:, :, b * S:(b + 1) * S], t), bank[4][:, 0:S]).then_inc(s["ctx_copied"], 1)

            def pair(t, last):
                for i in range(TILES):
                    row_max(t, i)
                    if i:
                        normalise(t, i - 1)
                    if not last:
                        if i == 2:
                            copy_rT(t + 1)
                        if i == 3:
                            copy_F(t + 1)
                        if i == 5:
                            copy_B(t + 1)
                            fold_lo(t + 1)
                    if i == 7:
                        copy_ctx(t, 0)
                    invert(t, i)
                normalise(t, TILES - 1)
                if not last:
                    for h in range(2):
                        q_lo(t + 1, h)
                copy_ctx(t, 1)

            with dve.Fori(0, HP - 1) as t:
                pair(t, False)
            pair(HP - 1, True)

            hold("gain_done", 1)
            for tt in range(NT):
                hold("out_made", tt + 1)
                v.scalar_tensor_tensor(out=x1[:, tt, :], in0=bank[tt % 2][:, 0:DIM], scalar=gain[:, 0:1],
                                       in1=x_sb[:, tt, :], op0=ALU.mult, op1=ALU.add).then_inc(s["x1_made"], 1)
                hold("x1_made", tt + 1)
                v.bn_stats(stats[:, tt, :], x1[:, tt, :]).then_inc(s["stat2"], 1)
                hold("stat2", tt + 1)
                v.bn_aggr(meanvar[:, tt, :], stats[:, tt, :]).then_inc(s["mv2"], 1)
                hold("sd2", tt + 1)
                v.reciprocal(rstd[:, tt:tt + 1], stdev[:, tt:tt + 1]).then_inc(s["rstd2"], 1)
                hold("rstd2", tt + 1)
                v.tensor_scalar(normed[:, tt, :], x1[:, tt, :], meanvar[:, tt, 0:1], rstd[:, tt:tt + 1],
                                ALU.subtract, ALU.mult).then_inc(s["norm2"], 1)
                if tt:
                    split_nT_lo(tt - 1, 4 + (tt - 1) % 2, "xhi2", "xlo2")
            split_nT_lo(NT - 1, 4 + (NT - 1) % 2, "xhi2", "xlo2")

            hold("logits_made", 1)
            v.tensor_copy(logit[:, :, :], bank[2][:, 0:NT * E].rearrange("p (t e) -> p t e", t=NT))\
                .then_inc(s["logits_copied"], 1)
            hold("logits_copied", 1)
            for tt in range(NT):
                v.max(top8[:, tt, :], logit[:, tt, :]).then_inc(s["top_made"], 1)
            hold("top_made", NT)
            v.tensor_tensor(shifted[:, :, :], logit[:, :, :], top8[:, :, 0:1].to_broadcast([P, NT, E]),
                            ALU.subtract).then_inc(s["shift_made"], 1)
            for tt in range(NT):
                v.match_replace(cut[:, tt, :], top8[:, tt, :], logit[:, tt, :], -3.0e38).then_inc(s["cut_made"], 1)
            hold("cut_made", NT)
            v.tensor_tensor(chosen[:, :, :], cut[:, :, :], logit[:, :, :], ALU.not_equal).then_inc(s["chosen_made"], 1)
            hold("chosen_made", 1)
            hold("expl_made", 1)
            v.tensor_tensor(picked[:, :, :], expl[:, :, :], chosen[:, :, :], ALU.mult).then_inc(s["picked_made"], 1)
            hold("picked_made", 1)
            v.tensor_reduce(psumw[:, :], picked[:, :, :], AX, ALU.add).then_inc(s["sum_made"], 1)
            hold("sum_made", 1)
            v.reciprocal(pinv[:, :], psumw[:, :]).then_inc(s["pinv_made"], 1)
            hold("pinv_made", 1)
            v.tensor_tensor(route[:, :, :], picked[:, :, :], pinv[:, :].unsqueeze(2).to_broadcast([P, NT, E]),
                            ALU.mult).then_inc(s["route_made"], 1)

            def inner(j, q, first=False, weight=None):
                hold("silu_made", q + 1)
                hold("up_mm", q + 1)
                v.tensor_tensor(gu[j % 2][:, :], act_g[j % 2][:, :], bank[2 + j % 2][:, :],
                                ALU.mult).then_inc(s["gu_made"], 1)
                if weight is None:
                    hold("weight_mm", q + 1)
                hold("gu_made", q + 1)
                v.tensor_tensor(weighted[j % 2][:, :], gu[j % 2][:, :],
                                bank[4 + j % 2][:, :] if weight is None else weight, ALU.mult)\
                    .then_inc(s["weighted_made"], 1)
                if not first:
                    hold("down_mm", q - 1)
                hold("weighted_made", q + 1)
                v.tensor_copy(in_hi[j % 2][:, :], weighted[j % 2][:, :]).then_inc(s["in_hi_made"], 1)
                hold("in_hi_made", q + 1)
                v.tensor_tensor(in_lo[j % 2][:, :], weighted[j % 2][:, :], in_hi[j % 2][:, :].bitcast(F32),
                                ALU.subtract).then_inc(s["in_ready"], 1)

            hold("shared_g_made", 1)
            inner(0, 0, first=True, weight=shared_g[:, :])
            hold("routeT_hi", 1)
            v.tensor_tensor(routeT[E:2 * E, :], bank[3][0:E, :], routeT[0:E, :].bitcast(F32),
                            ALU.subtract).then_inc(s["routeT_lo"], 1)
            inner(1, 1, first=True)
            for q in range(2, RING + 1):
                inner(q, q)
            with dve.Fori(1, (NP - 1) // RING) as u:
                for j in range(1, RING + 1):
                    inner(j, u * RING + j)
            hold("down_mm", NP)
            v.tensor_copy(outT[:, 1, :], bank[7][:, :]).then_inc(s["outT_copied"], 1)
            for tt in range(NT):
                hold("outT_t", tt + 1)
                v.scalar_tensor_tensor(out=fin[:, tt, :], in0=bank[tt][:, 0:DIM], scalar=gain[:, 1:2],
                                       in1=x1[:, tt, :], op0=ALU.mult, op1=ALU.add).then_inc(s["fin_made"], 1)

        @block.tensor
        def _(pe):
            mm = nc.tensor.matmul

            def hold(name, n):
                pe.wait_ge(s[name], n)

            def fold_r(t):
                hold("fold_loaded", t * 32 + 32)
                for c in range(2):
                    for h in range(2):
                        at = (2 * h + c) * (R + HK)
                        last = mm(bank[6][R * h:R * h + R, 0:HK], raw_q[:, at:at + R], raw_q[:, at + R:at + R + HK],
                                  start=(c == 0), stop=(c == 1))
                last.then_inc(s["rT_made"], 1)

            def fold_f(t, b_free=None):
                hold("rT_copied", t + 1)
                if b_free is not None:
                    hold("B_copied", b_free)
                for h in range(2):
                    last = mm(bank[6 + h][:, 0:DC], rT[R * h:R * h + R, :], raw_kv[R * h:R * h + R, 0:DC],
                              start=True, stop=True)
                last.then_inc(s["F_made"], 1)

            def fold_ab(t):
                hold("F_copied", 2 * t + 2)
                for h in range(2):
                    at = DC + h * PER_HEAD
                    for c in range(NC):
                        last = mm(bank[6][:, c * P + h * DC:c * P + (h + 1) * DC], raw_kv[:, at + c * P:at + (c + 1) * P],
                                  foldF[:, h, :], start=True, stop=True)
                last.then_inc(s["A_made"], 1)
                for h in range(2):
                    at = DC + h * PER_HEAD + DIM
                    last = mm(bank[7][DC * h:DC * h + DC, 0:DIM], raw_kv[:, at:at + DC],
                              raw_kv[:, at + DC:at + DC + DIM], start=True, stop=True)
                last.then_inc(s["B_made"], 1)

            parts = [(A_hi, nT_hi, c) for c in range(NC)] + [(A_hi, nT_lo, c) for c in range(NC)] \
                + [(A_lo, nT_hi, c) for c in range(NC)]

            def queries(t, which):
                if which == 0:
                    hold("A_hi_made", t + 1)
                    hold("A_lo_made", t + 1)
                for n in range(3 * which, 3 * which + 3):
                    w, y, c = parts[n]
                    last = mm(bank[5][:, :], w[:, c, :], y[:, c, :], start=(n == 0), stop=(n == 5))
                if which:
                    last.then_inc(s["q_made"], 1)

            fold_r(0)
            fold_f(0)
            hold("con_loaded", 16)
            for b in range(B):
                hold("rope_done", b + 1)
                for c in range(NL):
                    last = nc.tensor.transpose(bank[b][:, c * P:(c + 1) * P],
                                               kv[:, b * NL + c, :, :].rearrange("p a d -> p (a d)"), ident)
                last.then_inc(s["kT_made"], 1)

            def transpose_normed(tt, b, norm, done):
                hold(norm, tt + 1)
                for c in range(NC):
                    last = nc.tensor.transpose(bank[b][:, c * P:(c + 1) * P], normed[:, tt, c * P:(c + 1) * P], ident)
                last.then_inc(s[done], 1)

            for tt in range(NT):
                if tt >= 2:
                    hold("xlo1", tt - 1)
                transpose_normed(tt, 2 + tt % 2, "norm1", "xT1")
            fold_ab(0)
            hold("xlo1", NT)
            queries(0, 0)
            queries(0, 1)
            hold("k_lo", B)

            def scores(t, i):
                b, h, sc = tile_of(i)
                if i % (2 * NS) % NS == 0 and i < 2 * NS:
                    hold("q_lo", 2 * t + h + 1)
                rows = slice(b * S + sc * P, b * S + (sc + 1) * P)
                mm(bank[i % 2][:, :], Q[h][:, rows], K_hi[:, b, :], start=True, stop=False)
                mm(bank[i % 2][:, :], Q[h][:, rows], K_lo[:, b, :], start=False, stop=True).then_inc(s["scored"], 1)

            def transposes(t, i):
                hold("normalised", t * TILES + i + 1)
                for c in range(NL):
                    last = nc.tensor.transpose(bank[2 + i % 2][:, c * P:(c + 1) * P], prob[i % 4][:, c * P:(c + 1) * P],
                                               ident)
                last.then_inc(s["transposed"], 1)

            def attend(t, b):
                hold("probT_copied", t * TILES + (b + 1) * 2 * NS)
                for c in range(NL):
                    for h in range(2):
                        last = mm(bank[4][DC * h:DC * h + DC, 0:S], kv[:, b * NL + c, 0, :], probT[b][h][:, c, :],
                                  start=(c == 0), stop=(c == NL - 1))
                last.then_inc(s["attended"], 1)

            def pair(t, first, last):
                for i in range(TILES):
                    if not first or i >= 2:
                        hold("exp_made", t * TILES + i - 1)
                    scores(t, i)
                    if i >= 2:
                        if not first or i >= 4:
                            hold("probT_copied", t * TILES + i - 3)
                        transposes(t, i - 2)
                    if not last:
                        if i == 2:
                            fold_r(t + 1)
                        if i == 3:
                            fold_f(t + 1, t + 1)
                        if i == 4:
                            fold_ab(t + 1)
                    if i == 6:
                        if not first:
                            hold("ctx_copied", t * B)
                        attend(t, 0)
                if not last:
                    queries(t + 1, 0)
                hold("probT_copied", t * TILES + TILES - 3)
                transposes(t, TILES - 2)
                if not last:
                    queries(t + 1, 1)
                hold("probT_copied", t * TILES + TILES - 2)
                transposes(t, TILES - 1)
                hold("ctx_copied", t * B + 1)
                attend(t, 1)

            pair(0, True, False)
            with pe.Fori(1, HP - 1) as t:
                pair(t, False, False)
            pair(HP - 1, False, True)

            hold("ctx_copied", HP * B)
            hold("B_copied", HP)
            for tt in range(NT):
                if tt >= 2:
                    hold("x1_made", tt - 1)
                for p in range(HP):
                    last = mm(bank[tt % 2][:, 0:DIM], ctxT[:, p, tt * P:(tt + 1) * P], Bout[:, p, :],
                              start=(p == 0), stop=(p == HP - 1))
                last.then_inc(s["out_made"], 1)
                if tt:
                    if tt >= 3:
                        hold("xlo2", tt - 2)
                    transpose_normed(tt - 1, 4 + (tt - 1) % 2, "norm2", "xT2")
            hold("xlo2", NT - 2)
            transpose_normed(NT - 1, 4 + (NT - 1) % 2, "norm2", "xT2")
            hold("xlo2", NT)

            hold("gate_lo", 1)
            for tt in range(NT):
                rows = slice(tt * P, (tt + 1) * P)
                n = 0
                for c in range(NC):
                    for y, g in ((nT_hi, 0), (nT_hi, 1), (nT_lo, 0)):
                        last = mm(bank[2][:, tt * E:(tt + 1) * E], y[:, c, rows], gate_hl[:, c, g, :],
                                  start=(n == 0), stop=(n == 3 * NC - 1))
                        n += 1
            last.then_inc(s["logits_made"], 1)

            def three_parts(dst, hi, lo, done):
                n = 0
                for c in range(NC):
                    for w, y in ((hi(c), nT_hi), (hi(c), nT_lo), (lo(c), nT_hi)):
                        last = mm(dst, w, y[:, c, :], start=(n == 0), stop=(n == 3 * NC - 1))
                        n += 1
                last.then_inc(s[done], 1)

            def gate_up(j, q, free=True):
                slot = j % RING
                hold("w_lo", q + 1)
                for k, (b, done, used) in enumerate(((j % 2, "gate_mm", "silu_made"), (2 + j % 2, "up_mm", "gu_made"))):
                    if free:
                        hold(used, q - 1)
                    three_parts(bank[b][:, :],
                                lambda c: ffn_hi[slot][:, (2 * c + k) * P:(2 * c + k + 1) * P],
                                lambda c: ffn_lo[slot][:, (2 * c + k) * P:(2 * c + k + 1) * P], done)

            def weight(j, q, free=True):
                hold("pick_made", q)
                if free:
                    hold("weighted_made", q - 1)
                mm(bank[4 + j % 2][:, :], pick[j % RING][:, :], routeT[:, :], start=True,
                   stop=True).then_inc(s["weight_mm"], 1)

            def down(j, q, first=False, last_pair=False):
                hold("in_ready", q + 1)
                slot = j % RING
                for c in range(NC):
                    rows = slice(GU + c * P, GU + (c + 1) * P)
                    for n, (w, y) in enumerate(((ffn_hi, in_hi), (ffn_hi, in_lo), (ffn_lo, in_hi))):
                        last = mm(bank[6 + c][:, :], w[slot][:, rows], y[j % 2][:, :], start=(first and n == 0),
                                  stop=(last_pair and n == 2), skip_group_check=True)
                last.then_inc(s["down_mm"], 1)

            hold("logits_copied", 1)
            hold("g1_rest", 1)
            three_parts(bank[4][:, :], lambda c: g1_hi[:, c, :], lambda c: g1_lo[:, c, :], "weight_mm")
            gate_up(0, 0, free=False)
            for tt in range(NT):
                hold("route_made", 1)
                last = nc.tensor.transpose(bank[3][0:E, tt * P:(tt + 1) * P], route[:, tt, :], ident)
            last.then_inc(s["routeT_made"], 1)
            hold("routeT_lo", 1)
            gate_up(1, 1, free=False)
            weight(1, 1, free=False)
            down(0, 0, first=True)
            for q in range(2, RING + 1):
                gate_up(q, q)
                weight(q, q)
                down(q - 1, q - 1)
            with pe.Fori(1, (NP - 1) // RING) as u:
                for j in range(1, RING + 1):
                    gate_up(j, u * RING + j)
                    weight(j, u * RING + j)
                    down(j - 1, u * RING + j - 1)
            down(NP - 1, NP - 1, last_pair=True)

            hold("outT_copied", 2)
            hold("in_ready", NP)
            for tt in range(NT):
                for c in range(NC):
                    last = nc.tensor.transpose(bank[tt][:, c * P:(c + 1) * P], outT[:, c, tt * P:(tt + 1) * P], ident)
                last.then_inc(s["outT_t"], 1)


def kernel(x, ctx_512, g_xattn, g_ffn, L0_xattn_Wq, L0_xattn_w_kc_q, L0_xattn_w_kc_kv, L0_xattn_W_qr, L0_xattn_W_kr,
           L0_xattn_Wo, L0_ffn_gate_w, L0_ffn_gu_w, L0_ffn_dp_w, L0_ffn_sh_gate_w, L0_ffn_sh_up_w, L0_ffn_sh_down_w,
           L0_ffn_sh_gate1_w):
    import numpy as np
    import concourse.bacc as bacc
    from concourse.bass_utils import run_bass_kernel_spmd

    (x, ctx_512, g_xattn, g_ffn, Wq, kcq, kckv, Wqr, Wkr, Wo, gate, gu, dp, shg, shu, shd, shg1) = [
        np.asarray(a) for a in (x, ctx_512, g_xattn, g_ffn, L0_xattn_Wq, L0_xattn_w_kc_q, L0_xattn_w_kc_kv,
                                L0_xattn_W_qr, L0_xattn_W_kr, L0_xattn_Wo, L0_ffn_gate_w, L0_ffn_gu_w, L0_ffn_dp_w,
                                L0_ffn_sh_gate_w, L0_ffn_sh_up_w, L0_ffn_sh_down_w, L0_ffn_sh_gate1_w)]
    f32 = np.float32

    freq = f32(1.0) / f32(10000.0) ** (np.arange(0, DC, 2, dtype=f32) / f32(DC))
    angle = np.arange(L, dtype=f32)[:, None] * freq[None, :]
    cos = np.repeat(np.cos(angle), 2, axis=-1)
    sin = np.repeat(np.sin(angle), 2, axis=-1)
    sin = np.concatenate([-sin[:, :DC // 2], sin[:, DC // 2:]], axis=-1)
    rows = lambda a: a.reshape(NL, P, DC).transpose(1, 0, 2).reshape(P, NL * DC)
    consts = np.concatenate([np.eye(P, dtype=f32), rows(cos), rows(sin),
                             np.concatenate([np.eye(E, dtype=f32)] * 2)], axis=1).astype(f32)

    x_in = x.reshape(NT, P, DIM).transpose(1, 0, 2)
    ctx_in = ctx_512.reshape(B, NL, P, DC).transpose(2, 0, 1, 3)
    gains = np.broadcast_to(np.concatenate([g_xattn, g_ffn])[None, :], (P, 2))
    fq = np.concatenate([Wqr, kcq.transpose(0, 2, 1)], axis=2)
    fq = fq.reshape(HP, 2, 2, QH, R + HK).transpose(0, 3, 1, 2, 4).reshape(HP, QH, W1COLS)
    fh = np.concatenate([Wq.reshape(H, HK, DIM), kckv, Wo.T.reshape(H, HK, DIM)], axis=2)
    fh = fh.reshape(HP, 2, HK, PER_HEAD).transpose(0, 2, 1, 3).reshape(HP, P, 2 * PER_HEAD)
    fkv = np.concatenate([Wkr.transpose(0, 2, 1).reshape(HP, P, DC), fh], axis=2)
    by_chunk = lambda a: a.T.reshape(NC, P, -1).transpose(1, 0, 2)
    gate_in = by_chunk(gate)
    g1_in = np.broadcast_to(by_chunk(shg1), (P, NC, P))
    gu_sh = np.zeros((2, 2, EI, DIM), f32)
    gu_sh[0, 0], gu_sh[1, 0] = shg, shu
    gu_all = gu.reshape(EP, 2, 2, EI, DIM).transpose(0, 2, 1, 3, 4)
    gu_all = np.concatenate([gu_sh[None], gu_all]).reshape(NP, 2, P, NC, P).transpose(0, 4, 3, 1, 2)
    dp_sh = np.zeros((2, EI, DIM), f32)
    dp_sh[0] = shd.T
    dp_all = np.concatenate([dp_sh[None], dp.transpose(0, 2, 1).reshape(EP, 2, EI, DIM)]).reshape(NP, P, DIM)
    experts = np.concatenate([gu_all.reshape(NP, P, GU), dp_all], axis=2)

    arrays = {"x": x_in, "ctx": ctx_in, "consts": consts, "gains": gains, "w_fold_q": fq, "w_fold_kv": fkv,
              "gate_w": gate_in, "shared_gate1": g1_in, "w_experts": experts}
    nc = bacc.Bacc("TRN2", target_bir_lowering=False, num_devices=1)
    ins, args = {}, []
    for name, a in arrays.items():
        a = np.ascontiguousarray(a)
        ins[f"in_{name}"] = a
        args.append(nc.dram_tensor(f"in_{name}", a.shape, mybir.dt.from_np(a.dtype), kind="ExternalInput").ap())
    out = nc.dram_tensor("result", (TOK, DIM), F32, kind="ExternalOutput").ap()
    gated_cross_attention_moe(nc, *args, out.rearrange("(t p) c -> p t c", p=P))
    r = run_bass_kernel_spmd(nc, [ins], core_ids=[0])
    return r.results[0]["result"].reshape(B, S, DIM)
```

```python
from contextlib import ExitStack

import concourse.bass as bass
from concourse import mybir
from concourse.alu_op_type import AluOpType as ALU

F32 = mybir.dt.float32
F32R = mybir.dt.float32r
ACT = mybir.ActivationFunctionType
AX = mybir.AxisListType.X

P = 128
B, S, DIM = 2, 256, 256
L, DC = 512, 64
H, HK, CQ, R = 16, 128, 192, 64
E, EI, TOPK = 64, 64, 8
LN_EPS = 1e-5

TOK = B * S
NT = TOK // P
NC = DIM // P
NS = S // P
NL = L // P
HP = H // 2
QH = CQ // 2
TILES = B * 2 * NS
EP = E // 2
NP = EP + 1
W1COLS = 2 * 2 * (R + HK)
W2COLS = DC + 2 * DIM
W3COLS = 2 * (DC + DIM)
GU = NC * 2 * P
FW = GU + DIM
RING = 4
CI, CC, CS, CZ = 0, P, P + NL * DC, P + 2 * NL * DC
CONSTS = CZ + E


def gated_cross_attention_moe(nc, x, ctx, consts, gains, w_fold_r, w_fold_a, w_fold_b, gate_w, shared_gate1, w_experts, out):
    with ExitStack() as stack:
        def sb(name, shape, dt=F32):
            return stack.enter_context(nc.sbuf_tensor(name, shape, dt))

        def sem(name):
            return stack.enter_context(nc.semaphore(name))

        bank = [stack.enter_context(nc.psum_tensor(f"bank{i}", [P, 512], F32)) for i in range(8)]

        x_sb = sb("x_sb", [P, NT, DIM])
        ctx_sb = sb("ctx_sb", [P, B, NL, DC])
        con = sb("con", [P, CONSTS])
        gain_raw = sb("gain_raw", [P, 2])
        gain = sb("gain", [P, 2])
        eps = sb("eps", [P, 1])
        gate_raw = sb("gate_raw", [P, NC, E])
        gate_hl = sb("gate_hl", [P, NC, 2, E], F32R)
        g1_raw = sb("g1_raw", [P, NC, P])
        g1_hi = sb("g1_hi", [P, NC, P], F32R)
        g1_lo = sb("g1_lo", [P, NC, P], F32R)

        stats = sb("stats", [P, NT, 6])
        meanvar = sb("meanvar", [P, NT, 2])
        stdev = sb("stdev", [P, NT])
        rstd = sb("rstd", [P, NT])
        normed = sb("normed", [P, NT, DIM])
        nT_hi = sb("nT_hi", [P, NC, TOK], F32R)
        nT_lo = sb("nT_lo", [P, NC, TOK], F32R)

        kv = sb("kv", [P, B * NL, 2, DC])
        rot = sb("rot", [P, B * NL, DC])
        K_hi = sb("K_hi", [P, B, L], F32R)
        K_lo = sb("K_lo", [P, B, L], F32R)

        raw_r = sb("raw_r", [QH, W1COLS])
        raw_a = sb("raw_a", [P, W2COLS])
        raw_b = sb("raw_b", [P, W3COLS])
        rT = sb("rT", [P, HK])
        foldF = sb("foldF", [P, 2, DC])
        A_hi = sb("A_hi", [P, NC, P], F32R)
        A_lo = sb("A_lo", [P, NC, P], F32R)
        Bout = sb("Bout", [P, HP, DIM])
        Q = [sb(f"Q{h}", [P, TOK], F32R) for h in range(2)]
        nmax = sb("nmax", [P, TILES])
        rsum = sb("rsum", [P, TILES])
        rinv = sb("rinv", [P, TILES])
        prob = [sb(f"prob{i}", [P, L]) for i in range(4)]
        probT = [[sb(f"probT{b}{h}", [P, NL, S]) for h in range(2)] for b in range(B)]
        ctxT = sb("ctxT", [P, HP, TOK])

        x1 = sb("x1", [P, NT, DIM])
        logit = sb("logit", [P, NT, E])
        top8 = sb("top8", [P, NT, TOPK])
        cut = sb("cut", [P, NT, E])
        shifted = sb("shifted", [P, NT, E])
        chosen = sb("chosen", [P, NT, E])
        expl = sb("expl", [P, NT, E])
        picked = sb("picked", [P, NT, E])
        psumw = sb("psumw", [P, NT])
        pinv = sb("pinv", [P, NT])
        route = sb("route", [P, NT, E])
        routeT = sb("routeT", [P, TOK], F32R)

        ffn_raw = [sb(f"ffn_raw{i}", [P, FW]) for i in range(RING)]
        ffn_hi = [sb(f"ffn_hi{i}", [P, FW], F32R) for i in range(RING)]
        ffn_lo = [sb(f"ffn_lo{i}", [P, FW], F32R) for i in range(RING)]
        pick = [sb(f"pick{i}", [P, P], F32R) for i in range(RING)]
        act_g = [sb(f"act_g{i}", [P, TOK]) for i in range(2)]
        shared_g = sb("shared_g", [P, TOK])
        gu = [sb(f"gu{i}", [P, TOK]) for i in range(2)]
        weighted = [sb(f"weighted{i}", [P, TOK]) for i in range(2)]
        in_hi = [sb(f"in_hi{i}", [P, TOK], F32R) for i in range(2)]
        in_lo = [sb(f"in_lo{i}", [P, TOK], F32R) for i in range(2)]
        outT = sb("outT", [P, NC, TOK])
        fin = sb("fin", [P, NT, DIM])

        ident = con[:, CI:CI + P]
        cos = con[:, CC:CC + NL * DC].rearrange("p (l d) -> p l d", l=NL)
        sin = con[:, CS:CS + NL * DC].rearrange("p (l d) -> p l d", l=NL)
        stacked = con[:, CZ:CZ + E]

        names = """x_loaded ctx_loaded con_loaded raw_r_loaded raw_a_loaded raw_b_loaded small_loaded out_stored
            eps_set stat1 mv1 sd1 rstd1 norm1 xT1 xhi1 xlo1
            rope_cos rope_sin rope_done kT_made k_hi k_lo
            rT_made rT_copied F_made F_copied A_made A_hi_made A_lo_made B_made B_copied
            q_made q_hi q_lo scored max_made exp_made inv_made normalised transposed probT_copied
            attended ctx_copied gain_made gain_done
            out_made x1_made stat2 mv2 sd2 rstd2 norm2 xT2 xhi2 xlo2
            gate_hi gate_lo g1_split g1_rest logits_made logits_copied top_made cut_made shift_made chosen_made expl_made
            picked_made sum_made pinv_made route_made routeT_made routeT_hi routeT_lo
            w_hi w_lo pick_made gate_mm up_mm weight_mm silu_made shared_g_made gu_made weighted_made in_hi_made
            in_ready down_mm outT_copied outT_t fin_made""".split()
        s = {n: sem(n) for n in names}
        ffn_loaded = [sem(f"ffn_loaded{i}") for i in range(RING)]

        block = stack.enter_context(nc.Block())

        wr_r = w_fold_r.rearrange("t p n -> p t n")
        wa_r = w_fold_a.rearrange("t p n -> p t n")
        wb_r = w_fold_b.rearrange("t p n -> p t n")
        wf_r = w_experts.rearrange("t p n -> p t n")

        def tile_of(i):
            return i // (2 * NS), i // NS % 2, i % NS

        def dyn(ap3, t):
            return ap3[:, bass.ds(t, 1), :].rearrange("p a n -> p (a n)")

        @block.sync
        def _(sp):
            def load_r(t):
                sp.dma_start(raw_r[:, :], dyn(wr_r, t)).then_inc(s["raw_r_loaded"], 16)

            def load_a(t):
                sp.dma_start(raw_a[:, :], dyn(wa_r, t)).then_inc(s["raw_a_loaded"], 16)

            def load_b(t):
                sp.dma_start(raw_b[:, :], dyn(wb_r, t)).then_inc(s["raw_b_loaded"], 16)

            sp.dma_start(x_sb[:, :, :], x).then_inc(s["x_loaded"], 16)
            load_r(0)
            load_a(0)
            sp.dma_start(con[:, :], consts).then_inc(s["con_loaded"], 16)
            sp.dma_start(ctx_sb[:, :, :, :], ctx).then_inc(s["ctx_loaded"], 16)
            load_b(0)
            sp.dma_start(gain_raw[:, :], gains).then_inc(s["small_loaded"], 16)
            sp.dma_start(gate_raw[:, :, :], gate_w).then_inc(s["small_loaded"], 16)
            sp.dma_start(g1_raw[:, :, :], shared_gate1).then_inc(s["small_loaded"], 16)
            for q in range(RING):
                sp.dma_start(ffn_raw[q][:, :], dyn(wf_r, q)).then_inc(ffn_loaded[q], 16)
            with sp.Fori(1, HP) as t:
                sp.wait_ge(s["rT_made"], t)
                load_r(t)
                sp.wait_ge(s["A_made"], t)
                load_a(t)
                sp.wait_ge(s["B_made"], t)
                load_b(t)
            with sp.Fori(0, (NP - 1 - RING) // RING) as u:
                for j in range(RING):
                    sp.wait_ge(s["w_lo"], u * RING + j + 1)
                    sp.dma_start(ffn_raw[j][:, :], dyn(wf_r, u * RING + j + RING)).then_inc(ffn_loaded[j], 16)
            for q in range(NP - 1 - (NP - 1) % RING, NP):
                sp.wait_ge(s["w_lo"], q - RING + 1)
                sp.dma_start(ffn_raw[q % RING][:, :], wf_r[:, q, :]).then_inc(ffn_loaded[q % RING], 16)
            for tt in range(NT):
                sp.wait_ge(s["fin_made"], tt + 1)
                sp.dma_start(out[:, tt, :], fin[:, tt, :]).then_inc(s["out_stored"], 16)
            sp.wait_ge(s["out_stored"], 16 * NT)

        @block.gpsimd
        def _(pool):
            def split_lo(slot, q):
                pool.wait_ge(s["w_hi"], q + 1)
                nc.gpsimd.tensor_tensor(ffn_lo[slot][:, :], ffn_raw[slot][:, :], ffn_hi[slot][:, :].bitcast(F32),
                                        ALU.subtract).then_inc(s["w_lo"], 1)

            pool.wait_ge(s["small_loaded"], 48)
            pool.wait_ge(s["gate_hi"], 1)
            nc.gpsimd.tensor_tensor(gate_hl[:, :, 1, :], gate_raw[:, :, :], gate_hl[:, :, 0, :].bitcast(F32),
                                    ALU.subtract).then_inc(s["gate_lo"], 1)
            pool.wait_ge(s["g1_split"], 1)
            nc.gpsimd.tensor_tensor(g1_lo[:, :, :], g1_raw[:, :, :], g1_hi[:, :, :].bitcast(F32),
                                    ALU.subtract).then_inc(s["g1_rest"], 1)
            for q in range(2):
                split_lo(q, q)
            with pool.Fori(0, (NP - 1) // RING - 1) as u:
                for j in range(RING):
                    split_lo((2 + j) % RING, u * RING + j + 2)
            for q in range(NP - 1 - RING + 2, NP):
                split_lo(q % RING, q)

        @block.scalar
        def _(act):
            def copy(dst, src, done):
                nc.scalar.activation(dst, src, ACT.Copy).then_inc(s[done], 1)

            act.wait_ge(s["mv1"], NT)
            nc.scalar.activation(stdev[:, :], meanvar[:, :, 1], ACT.Sqrt, bias=eps[:, 0:1]).then_inc(s["sd1"], 1)
            act.preload_act_table(ACT.Exp)

            def fold_hi(t):
                act.wait_ge(s["A_made"], t + 1)
                copy(A_hi[:, :, :], bank[6][:, 0:NC * P].rearrange("p (c n) -> p c n", c=NC), "A_hi_made")

            def split_nT_hi(tt, b, made, done):
                act.wait_ge(s[made], tt + 1)
                copy(nT_hi[:, :, tt * P:(tt + 1) * P], bank[b][:, 0:NC * P].rearrange("p (c n) -> p c n", c=NC), done)

            for b in range(B):
                act.wait_ge(s["kT_made"], b + 1)
                copy(K_hi[:, b, :], bank[b][:, :], "k_hi")
            for tt in range(NT):
                split_nT_hi(tt, 2 + tt % 2, "xT1", "xhi1")
            fold_hi(0)

            def q_hi(t, h):
                act.wait_ge(s["q_made"], t + 1)
                copy(Q[h][0:DC, :], bank[5][DC * h:DC * h + DC, :], "q_hi")

            for h in range(2):
                q_hi(0, h)
            act.wait_ge(s["small_loaded"], 48)
            copy(gate_hl[:, :, 0, :], gate_raw[:, :, :], "gate_hi")
            copy(g1_hi[:, :, :], g1_raw[:, :, :], "g1_split")
            nc.scalar.activation(gain[:, :], gain_raw[:, :], ACT.Tanh).then_inc(s["gain_done"], 1)

            def exponentials(t, i):
                act.wait_ge(s["max_made"], t * TILES + i + 1)
                nc.scalar.activation(prob[i % 4][:, :], bank[i % 2][:, :], ACT.Exp, bias=nmax[:, i:i + 1],
                                     accum_out=rsum[:, i:i + 1]).then_inc(s["exp_made"], 1)

            def copy_probT(t, i):
                b, h, sc = tile_of(i)
                act.wait_ge(s["transposed"], t * TILES + i + 1)
                copy(probT[b][h][:, :, sc * P:(sc + 1) * P], bank[2 + i % 2][:, :].rearrange("p (l n) -> p l n", l=NL),
                     "probT_copied")

            def copy_ctx(t, b):
                act.wait_ge(s["attended"], t * B + b + 1)
                copy(dyn(ctxT[:, :, b * S:(b + 1) * S], t), bank[4][:, 0:S], "ctx_copied")

            def pair(t, first, last):
                for i in range(TILES):
                    if i == 0 and not first:
                        q_hi(t, 1)
                    if i == 6 and not last:
                        q_hi(t + 1, 0)
                    exponentials(t, i)
                    if i >= 2:
                        copy_probT(t, i - 2)
                    elif not first:
                        copy_probT(t - 1, TILES + i - 2)
                    if not first and i in (1, 5):
                        copy_ctx(t - 1, i // 4)
                    if not last:
                        if i == 3:
                            fold_hi(t + 1)

            pair(0, True, False)
            with act.Fori(1, HP - 1) as t:
                pair(t, False, False)
            pair(HP - 1, False, True)
            copy_probT(HP - 1, TILES - 2)
            copy_probT(HP - 1, TILES - 1)
            copy_ctx(HP - 1, 0)
            copy_ctx(HP - 1, 1)

            def weights_hi(slot, q):
                act.wait_ge(ffn_loaded[slot], (q // RING) * 16 + 16)
                copy(ffn_hi[slot][:, :], ffn_raw[slot][:, :], "w_hi")

            weights_hi(0, 0)
            weights_hi(1, 1)
            for tt in range(NT):
                act.wait_ge(s["mv2"], tt + 1)
                nc.scalar.activation(stdev[:, tt:tt + 1], meanvar[:, tt, 1:2], ACT.Sqrt,
                                     bias=eps[:, 0:1]).then_inc(s["sd2"], 1)
                if tt:
                    split_nT_hi(tt - 1, 4 + (tt - 1) % 2, "xT2", "xhi2")
            act.preload_act_table(ACT.Exp)
            split_nT_hi(NT - 1, 4 + (NT - 1) % 2, "xT2", "xhi2")
            act.wait_ge(s["shift_made"], 1)
            nc.scalar.activation(expl[:, :, :], shifted[:, :, :], ACT.Exp).then_inc(s["expl_made"], 1)
            act.wait_ge(s["weight_mm"], 1)
            nc.scalar.activation(shared_g[:, :], bank[4][:, :], ACT.Sigmoid).then_inc(s["shared_g_made"], 1)
            act.preload_act_table(ACT.Silu)

            def silu(j, q, first=False):
                act.wait_ge(s["gate_mm"], q + 1)
                if not first:
                    act.wait_ge(s["gu_made"], q - 1)
                nc.scalar.activation(act_g[j % 2][:, :], bank[j % 2][:, :], ACT.Silu).then_inc(s["silu_made"], 1)

            def make_pick(slot, q):
                src = stacked[:, bass.ds((q - 1) * 2, 2)]
                nc.scalar.activation(pick[slot][:, :].rearrange("p (e n) -> p e n", e=2),
                                     src.unsqueeze(2).to_broadcast([P, 2, EI]), ACT.Copy).then_inc(s["pick_made"], 1)

            def ffn_pair(j, q):
                silu(j, q)

            silu(0, 0, first=True)
            act.wait_ge(s["routeT_made"], 1)
            copy(routeT[0:E, :], bank[5][0:E, :], "routeT_hi")
            make_pick(1, 1)
            make_pick(2, 2)
            weights_hi(2, 2)

            def step(j, q, ahead=True):
                silu(j, q)
                if ahead:
                    act.wait_ge(s["down_mm"], q - 1)
                    slot = (j + 2) % RING
                    act.wait_ge(ffn_loaded[slot], ((j + 2) // RING) * 16 + (q - j) * (16 // RING) + 16)
                    copy(ffn_hi[slot][:, :], ffn_raw[slot][:, :], "w_hi")
                    make_pick(slot, q + 2)

            silu(1, 1, first=True)
            act.wait_ge(ffn_loaded[3], 16)
            copy(ffn_hi[3][:, :], ffn_raw[3][:, :], "w_hi")
            make_pick(3, 3)
            for j in range(2, RING):
                step(j, j)
            step(RING, RING)
            with act.Fori(1, (NP - 1) // RING - 1) as u:
                for j in range(1, RING + 1):
                    step(j, u * RING + j)
            for q in range(NP - RING, NP):
                step((q - 1) % RING + 1 if False else q, q, ahead=q + 2 < NP)

            for c in range(NC):
                act.wait_ge(s["down_mm"], NP)
                if c == 0:
                    copy(outT[:, c, :], bank[6 + c][:, :], "outT_copied")

        @block.vector
        def _(dve):
            v = nc.vector

            def hold(name, n):
                dve.wait_ge(s[name], n)

            v.memset(eps[:, :], LN_EPS).then_inc(s["eps_set"], 1)
            hold("x_loaded", 16)
            for tt in range(NT):
                v.bn_stats(stats[:, tt, :], x_sb[:, tt, :]).then_inc(s["stat1"], 1)
            for tt in range(NT):
                hold("stat1", tt + 1)
                v.bn_aggr(meanvar[:, tt, :], stats[:, tt, :]).then_inc(s["mv1"], 1)
            hold("sd1", 1)
            v.reciprocal(rstd[:, :], stdev[:, :]).then_inc(s["rstd1"], 1)
            hold("rstd1", 1)
            for tt in range(NT):
                v.tensor_scalar(normed[:, tt, :], x_sb[:, tt, :], meanvar[:, tt, 0:1], rstd[:, tt:tt + 1],
                                ALU.subtract, ALU.mult).then_inc(s["norm1"], 1)
            hold("con_loaded", 16)
            hold("ctx_loaded", 16)
            half = DC // 2
            for b in range(B):
                rows = slice(b * NL, (b + 1) * NL)
                v.tensor_tensor(rot[:, rows, 0:half], ctx_sb[:, b, :, half:DC], sin[:, :, 0:half],
                                ALU.mult).then_inc(s["rope_sin"], 1)
                v.tensor_tensor(rot[:, rows, half:DC], ctx_sb[:, b, :, 0:half], sin[:, :, half:DC],
                                ALU.mult).then_inc(s["rope_sin"], 1)
                v.tensor_tensor(kv[:, rows, 0, :], ctx_sb[:, b, :, :], cos, ALU.mult).then_inc(s["rope_cos"], 1)
            for b in range(B):
                rows = slice(b * NL, (b + 1) * NL)
                hold("rope_sin", 2 * b + 2)
                hold("rope_cos", b + 1)
                v.tensor_tensor(kv[:, rows, 1, :], kv[:, rows, 0, :], rot[:, rows, :], ALU.add)
                v.tensor_tensor(kv[:, rows, 0, :], kv[:, rows, 0, :], rot[:, rows, :],
                                ALU.add).then_inc(s["rope_done"], 1)

            def copy_rT(t):
                hold("rT_made", t + 1)
                v.tensor_copy(rT[:, :], bank[6][:, 0:HK]).then_inc(s["rT_copied"], 1)

            def copy_F(t):
                hold("F_made", t + 1)
                v.tensor_copy(foldF[:, 0, :], bank[6][:, 0:DC]).then_inc(s["F_copied"], 1)
                v.tensor_copy(foldF[:, 1, :], bank[7][:, 0:DC]).then_inc(s["F_copied"], 1)

            def copy_B(t):
                hold("B_made", t + 1)
                v.tensor_copy(dyn(Bout, t), bank[7][:, DIM:2 * DIM]).then_inc(s["B_copied"], 1)

            def fold_lo(t):
                hold("A_hi_made", t + 1)
                v.tensor_tensor(A_lo[:, :, :], bank[6][:, 0:NC * P].rearrange("p (c n) -> p c n", c=NC),
                                A_hi[:, :, :].bitcast(F32), ALU.subtract).then_inc(s["A_lo_made"], 1)

            def q_lo(t, h):
                hold("q_hi", 2 * t + h + 1)
                v.tensor_tensor(Q[h][DC:P, :], bank[5][DC * h:DC * h + DC, :], Q[h][0:DC, :].bitcast(F32),
                                ALU.subtract).then_inc(s["q_lo"], 1)

            def split_nT_lo(tt, b, hi, done):
                hold(hi, tt + 1)
                v.tensor_tensor(nT_lo[:, :, tt * P:(tt + 1) * P],
                                bank[b][:, 0:NC * P].rearrange("p (c n) -> p c n", c=NC),
                                nT_hi[:, :, tt * P:(tt + 1) * P].bitcast(F32), ALU.subtract).then_inc(s[done], 1)

            copy_rT(0)
            copy_F(0)
            for b in range(B):
                hold("k_hi", b + 1)
                v.tensor_tensor(K_lo[:, b, :], bank[b][:, :], K_hi[:, b, :].bitcast(F32),
                                ALU.subtract).then_inc(s["k_lo"], 1)
            for tt in range(NT):
                split_nT_lo(tt, 2 + tt % 2, "xhi1", "xlo1")
            fold_lo(0)
            for h in range(2):
                q_lo(0, h)

            copy_B(0)

            def row_max(t, i):
                hold("scored", t * TILES + i + 1)
                v.tensor_reduce(nmax[:, i:i + 1], bank[i % 2][:, :], AX, ALU.max, negate=True).then_inc(s["max_made"], 1)

            def invert(t, i):
                hold("exp_made", t * TILES + i + 1)
                v.reciprocal(rinv[:, i:i + 1], rsum[:, i:i + 1]).then_inc(s["inv_made"], 1)

            def normalise(t, i):
                hold("inv_made", t * TILES + i + 1)
                v.tensor_scalar(prob[i % 4][:, :], prob[i % 4][:, :], rinv[:, i:i + 1], None,
                                ALU.mult).then_inc(s["normalised"], 1)

            def pair(t, first, last):
                for i in range(TILES):
                    row_max(t, i)
                    if i:
                        normalise(t, i - 1)
                    elif not first:
                        normalise(t - 1, TILES - 1)
                        q_lo(t, 1)
                    if not last:
                        if i == 0:
                            copy_rT(t + 1)
                        if i == 1:
                            copy_F(t + 1)
                        if i == 2:
                            copy_B(t + 1)
                        if i == 3:
                            fold_lo(t + 1)
                        if i == 6:
                            q_lo(t + 1, 0)
                    invert(t, i)

            pair(0, True, False)
            with dve.Fori(1, HP - 1) as t:
                pair(t, False, False)
            pair(HP - 1, False, True)
            normalise(HP - 1, TILES - 1)

            hold("gain_done", 1)
            for tt in range(NT):
                hold("out_made", tt + 1)
                v.scalar_tensor_tensor(out=x1[:, tt, :], in0=bank[tt % 2][:, 0:DIM], scalar=gain[:, 0:1],
                                       in1=x_sb[:, tt, :], op0=ALU.mult, op1=ALU.add).then_inc(s["x1_made"], 1)
                hold("x1_made", tt + 1)
                v.bn_stats(stats[:, tt, :], x1[:, tt, :]).then_inc(s["stat2"], 1)
                hold("stat2", tt + 1)
                v.bn_aggr(meanvar[:, tt, :], stats[:, tt, :]).then_inc(s["mv2"], 1)
                hold("sd2", tt + 1)
                v.reciprocal(rstd[:, tt:tt + 1], stdev[:, tt:tt + 1]).then_inc(s["rstd2"], 1)
                hold("rstd2", tt + 1)
                v.tensor_scalar(normed[:, tt, :], x1[:, tt, :], meanvar[:, tt, 0:1], rstd[:, tt:tt + 1],
                                ALU.subtract, ALU.mult).then_inc(s["norm2"], 1)
                if tt:
                    split_nT_lo(tt - 1, 4 + (tt - 1) % 2, "xhi2", "xlo2")
            split_nT_lo(NT - 1, 4 + (NT - 1) % 2, "xhi2", "xlo2")

            hold("logits_made", 1)
            v.tensor_copy(logit[:, :, :], bank[2][:, 0:NT * E].rearrange("p (t e) -> p t e", t=NT))\
                .then_inc(s["logits_copied"], 1)
            hold("logits_copied", 1)
            for tt in range(NT):
                v.max(top8[:, tt, :], logit[:, tt, :]).then_inc(s["top_made"], 1)
            hold("top_made", NT)
            v.tensor_tensor(shifted[:, :, :], logit[:, :, :], top8[:, :, 0:1].to_broadcast([P, NT, E]),
                            ALU.subtract).then_inc(s["shift_made"], 1)
            for tt in range(NT):
                v.match_replace(cut[:, tt, :], top8[:, tt, :], logit[:, tt, :], -3.0e38).then_inc(s["cut_made"], 1)
            hold("cut_made", NT)
            v.tensor_tensor(chosen[:, :, :], cut[:, :, :], logit[:, :, :], ALU.not_equal).then_inc(s["chosen_made"], 1)
            hold("chosen_made", 1)
            hold("expl_made", 1)
            v.tensor_tensor(picked[:, :, :], expl[:, :, :], chosen[:, :, :], ALU.mult).then_inc(s["picked_made"], 1)
            hold("picked_made", 1)
            v.tensor_reduce(psumw[:, :], picked[:, :, :], AX, ALU.add).then_inc(s["sum_made"], 1)
            hold("sum_made", 1)
            v.reciprocal(pinv[:, :], psumw[:, :]).then_inc(s["pinv_made"], 1)
            hold("pinv_made", 1)
            v.tensor_tensor(route[:, :, :], picked[:, :, :], pinv[:, :].unsqueeze(2).to_broadcast([P, NT, E]),
                            ALU.mult).then_inc(s["route_made"], 1)

            def inner(j, q, first=False, weight=None):
                hold("silu_made", q + 1)
                hold("up_mm", q + 1)
                v.tensor_tensor(gu[j % 2][:, :], act_g[j % 2][:, :], bank[2 + j % 2][:, :],
                                ALU.mult).then_inc(s["gu_made"], 1)
                if weight is None:
                    hold("weight_mm", q + 1)
                hold("gu_made", q + 1)
                v.tensor_tensor(weighted[j % 2][:, :], gu[j % 2][:, :],
                                bank[4 + j % 2][:, :] if weight is None else weight, ALU.mult)\
                    .then_inc(s["weighted_made"], 1)
                if not first:
                    hold("down_mm", q - 1)
                hold("weighted_made", q + 1)
                v.tensor_copy(in_hi[j % 2][:, :], weighted[j % 2][:, :]).then_inc(s["in_hi_made"], 1)
                hold("in_hi_made", q + 1)
                v.tensor_tensor(in_lo[j % 2][:, :], weighted[j % 2][:, :], in_hi[j % 2][:, :].bitcast(F32),
                                ALU.subtract).then_inc(s["in_ready"], 1)

            hold("shared_g_made", 1)
            inner(0, 0, first=True, weight=shared_g[:, :])
            hold("routeT_hi", 1)
            v.tensor_tensor(routeT[E:2 * E, :], bank[5][0:E, :], routeT[0:E, :].bitcast(F32),
                            ALU.subtract).then_inc(s["routeT_lo"], 1)
            inner(1, 1, first=True)
            for q in range(2, RING + 1):
                inner(q, q)
            with dve.Fori(1, (NP - 1) // RING) as u:
                for j in range(1, RING + 1):
                    inner(j, u * RING + j)
            hold("down_mm", NP)
            v.tensor_copy(outT[:, 1, :], bank[7][:, :]).then_inc(s["outT_copied"], 1)
            for tt in range(NT):
                hold("outT_t", tt + 1)
                v.scalar_tensor_tensor(out=fin[:, tt, :], in0=bank[tt][:, 0:DIM], scalar=gain[:, 1:2],
                                       in1=x1[:, tt, :], op0=ALU.mult, op1=ALU.add).then_inc(s["fin_made"], 1)

        @block.tensor
        def _(pe):
            mm = nc.tensor.matmul

            def hold(name, n):
                pe.wait_ge(s[name], n)

            def fold_r(t):
                hold("raw_r_loaded", t * 16 + 16)
                for c in range(2):
                    for h in range(2):
                        at = (2 * h + c) * (R + HK)
                        last = mm(bank[6][R * h:R * h + R, 0:HK], raw_r[:, at:at + R], raw_r[:, at + R:at + R + HK],
                                  start=(c == 0), stop=(c == 1))
                last.then_inc(s["rT_made"], 1)

            def fold_f(t):
                hold("rT_copied", t + 1)
                hold("raw_a_loaded", t * 16 + 16)
                for h in range(2):
                    last = mm(bank[6 + h][:, 0:DC], rT[R * h:R * h + R, :], raw_a[R * h:R * h + R, 0:DC],
                              start=True, stop=True)
                last.then_inc(s["F_made"], 1)

            def fold_a(t):
                hold("F_copied", 2 * t + 2)
                for h in range(2):
                    for c in range(NC):
                        at = DC + h * DIM + c * P
                        last = mm(bank[6][:, c * P + h * DC:c * P + (h + 1) * DC], raw_a[:, at:at + P],
                                  foldF[:, h, :], start=True, stop=True)
                last.then_inc(s["A_made"], 1)

            def fold_b(t, last_copied=True):
                hold("raw_b_loaded", t * 16 + 16)
                if last_copied:
                    hold("B_copied", t)
                for h in range(2):
                    at = h * (DC + DIM)
                    last = mm(bank[7][DC * h:DC * h + DC, DIM:2 * DIM], raw_b[:, at:at + DC],
                              raw_b[:, at + DC:at + DC + DIM], start=True, stop=True)
                last.then_inc(s["B_made"], 1)

            parts = [(A_hi, nT_hi, c) for c in range(NC)] + [(A_hi, nT_lo, c) for c in range(NC)] \
                + [(A_lo, nT_hi, c) for c in range(NC)]

            def queries(t, which):
                if which == 0:
                    hold("A_hi_made", t + 1)
                    hold("A_lo_made", t + 1)
                for n in range(3 * which, 3 * which + 3):
                    w, y, c = parts[n]
                    last = mm(bank[5][:, :], w[:, c, :], y[:, c, :], start=(n == 0), stop=(n == 5))
                if which:
                    last.then_inc(s["q_made"], 1)

            fold_r(0)
            fold_f(0)
            hold("con_loaded", 16)
            for b in range(B):
                hold("rope_done", b + 1)
                for c in range(NL):
                    last = nc.tensor.transpose(bank[b][:, c * P:(c + 1) * P],
                                               kv[:, b * NL + c, :, :].rearrange("p a d -> p (a d)"), ident)
                last.then_inc(s["kT_made"], 1)

            def transpose_normed(tt, b, norm, done):
                hold(norm, tt + 1)
                for c in range(NC):
                    last = nc.tensor.transpose(bank[b][:, c * P:(c + 1) * P], normed[:, tt, c * P:(c + 1) * P], ident)
                last.then_inc(s[done], 1)

            for tt in range(NT):
                if tt >= 2:
                    hold("xlo1", tt - 1)
                transpose_normed(tt, 2 + tt % 2, "norm1", "xT1")
            fold_a(0)
            hold("xlo1", NT)
            queries(0, 0)
            queries(0, 1)
            fold_b(0, last_copied=False)
            hold("k_lo", B)

            def scores(t, i):
                b, h, sc = tile_of(i)
                if b == 0 and sc == 0:
                    hold("q_lo", 2 * t + h + 1)
                rows = slice(b * S + sc * P, b * S + (sc + 1) * P)
                mm(bank[i % 2][:, :], Q[h][:, rows], K_hi[:, b, :], start=True, stop=False)
                mm(bank[i % 2][:, :], Q[h][:, rows], K_lo[:, b, :], start=False, stop=True).then_inc(s["scored"], 1)

            def transposes(t, i, free=True):
                if free:
                    hold("probT_copied", t * TILES + i - 1)
                hold("normalised", t * TILES + i + 1)
                for c in range(NL):
                    last = nc.tensor.transpose(bank[2 + i % 2][:, c * P:(c + 1) * P], prob[i % 4][:, c * P:(c + 1) * P],
                                               ident)
                last.then_inc(s["transposed"], 1)

            def attend(t, b, chunks, free=True):
                if chunks[0] == 0:
                    hold("probT_copied", t * TILES + (b + 1) * 2 * NS)
                    if free:
                        hold("ctx_copied", t * B + b)
                for c in chunks:
                    for h in range(2):
                        last = mm(bank[4][DC * h:DC * h + DC, 0:S], kv[:, b * NL + c, 0, :], probT[b][h][:, c, :],
                                  start=(c == 0), stop=(c == NL - 1))
                if chunks[-1] == NL - 1:
                    last.then_inc(s["attended"], 1)

            first_half, second_half = range(NL // 2), range(NL // 2, NL)

            def pair(t, first, last):
                for i in range(TILES):
                    if not first or i >= 2:
                        hold("exp_made", t * TILES + i - 1)
                    scores(t, i)
                    if not last and i == 0:
                        fold_r(t + 1)
                    if i >= 2:
                        transposes(t, i - 2, free=not first or i >= 4)
                    elif not first:
                        transposes(t - 1, TILES + i - 2)
                    if not last:
                        if i == 1:
                            fold_b(t + 1)
                            fold_f(t + 1)
                        if i == 2:
                            fold_a(t + 1)
                        if i == 5:
                            queries(t + 1, 0)
                            queries(t + 1, 1)
                    if not first and i in (3, 4):
                        attend(t - 1, 1, (first_half, second_half)[i - 3])
                    if i >= 6:
                        attend(t, 0, (first_half, second_half)[i - 6], free=not first)

            pair(0, True, False)
            with pe.Fori(1, HP - 1) as t:
                pair(t, False, False)
            pair(HP - 1, False, True)

            transposes(HP - 1, TILES - 2)
            transposes(HP - 1, TILES - 1)
            hold("B_copied", HP)
            for tt in range(NT):
                if tt == 1:
                    attend(HP - 1, 1, range(NL))
                hold("ctx_copied", (HP - 1) * B + tt // NS + 1)
                if tt >= 2:
                    hold("x1_made", tt - 1)
                for p in range(HP):
                    last = mm(bank[tt % 2][:, 0:DIM], ctxT[:, p, tt * P:(tt + 1) * P], Bout[:, p, :],
                              start=(p == 0), stop=(p == HP - 1))
                last.then_inc(s["out_made"], 1)
                if tt:
                    if tt >= 3:
                        hold("xlo2", tt - 2)
                    transpose_normed(tt - 1, 4 + (tt - 1) % 2, "norm2", "xT2")
            hold("xlo2", NT - 2)
            transpose_normed(NT - 1, 4 + (NT - 1) % 2, "norm2", "xT2")
            hold("xlo2", NT)

            hold("gate_lo", 1)
            for tt in range(NT):
                rows = slice(tt * P, (tt + 1) * P)
                n = 0
                for c in range(NC):
                    for y, g in ((nT_hi, 0), (nT_hi, 1), (nT_lo, 0)):
                        last = mm(bank[2][:, tt * E:(tt + 1) * E], y[:, c, rows], gate_hl[:, c, g, :],
                                  start=(n == 0), stop=(n == 3 * NC - 1))
                        n += 1
            last.then_inc(s["logits_made"], 1)

            def three_parts(dst, hi, lo, done):
                n = 0
                for c in range(NC):
                    for w, y in ((hi(c), nT_hi), (hi(c), nT_lo), (lo(c), nT_hi)):
                        last = mm(dst, w, y[:, c, :], start=(n == 0), stop=(n == 3 * NC - 1))
                        n += 1
                last.then_inc(s[done], 1)

            def gate_up(j, q, free=True):
                slot = j % RING
                hold("w_lo", q + 1)
                for k, (b, done, used) in enumerate(((j % 2, "gate_mm", "silu_made"), (2 + j % 2, "up_mm", "gu_made"))):
                    if free:
                        hold(used, q - 1)
                    three_parts(bank[b][:, :],
                                lambda c: ffn_hi[slot][:, (2 * c + k) * P:(2 * c + k + 1) * P],
                                lambda c: ffn_lo[slot][:, (2 * c + k) * P:(2 * c + k + 1) * P], done)

            def weight(j, q, free=True):
                hold("pick_made", q)
                if free:
                    hold("weighted_made", q - 1)
                mm(bank[4 + j % 2][:, :], pick[j % RING][:, :], routeT[:, :], start=True,
                   stop=True).then_inc(s["weight_mm"], 1)

            def down(j, q, first=False, last_pair=False):
                hold("in_ready", q + 1)
                slot = j % RING
                for c in range(NC):
                    rows = slice(GU + c * P, GU + (c + 1) * P)
                    for n, (w, y) in enumerate(((ffn_hi, in_hi), (ffn_hi, in_lo), (ffn_lo, in_hi))):
                        last = mm(bank[6 + c][:, :], w[slot][:, rows], y[j % 2][:, :], start=(first and n == 0),
                                  stop=(last_pair and n == 2), skip_group_check=True)
                last.then_inc(s["down_mm"], 1)

            hold("logits_copied", 1)
            hold("g1_rest", 1)
            three_parts(bank[4][:, :], lambda c: g1_hi[:, c, :], lambda c: g1_lo[:, c, :], "weight_mm")
            gate_up(0, 0, free=False)
            for tt in range(NT):
                hold("route_made", 1)
                last = nc.tensor.transpose(bank[5][0:E, tt * P:(tt + 1) * P], route[:, tt, :], ident)
            last.then_inc(s["routeT_made"], 1)
            gate_up(1, 1, free=False)
            hold("routeT_lo", 1)
            weight(1, 1, free=False)
            down(0, 0, first=True)
            for q in range(2, RING + 1):
                gate_up(q, q)
                weight(q, q)
                down(q - 1, q - 1)
            with pe.Fori(1, (NP - 1) // RING) as u:
                for j in range(1, RING + 1):
                    gate_up(j, u * RING + j)
                    weight(j, u * RING + j)
                    down(j - 1, u * RING + j - 1)
            down(NP - 1, NP - 1, last_pair=True)

            hold("outT_copied", 2)
            hold("in_ready", NP)
            for tt in range(NT):
                for c in range(NC):
                    last = nc.tensor.transpose(bank[tt][:, c * P:(c + 1) * P], outT[:, c, tt * P:(tt + 1) * P], ident)
                last.then_inc(s["outT_t"], 1)


def kernel(x, ctx_512, g_xattn, g_ffn, L0_xattn_Wq, L0_xattn_w_kc_q, L0_xattn_w_kc_kv, L0_xattn_W_qr, L0_xattn_W_kr,
           L0_xattn_Wo, L0_ffn_gate_w, L0_ffn_gu_w, L0_ffn_dp_w, L0_ffn_sh_gate_w, L0_ffn_sh_up_w, L0_ffn_sh_down_w,
           L0_ffn_sh_gate1_w):
    import numpy as np
    import concourse.bacc as bacc
    from concourse.bass_utils import run_bass_kernel_spmd

    (x, ctx_512, g_xattn, g_ffn, Wq, kcq, kckv, Wqr, Wkr, Wo, gate, gu, dp, shg, shu, shd, shg1) = [
        np.asarray(a) for a in (x, ctx_512, g_xattn, g_ffn, L0_xattn_Wq, L0_xattn_w_kc_q, L0_xattn_w_kc_kv,
                                L0_xattn_W_qr, L0_xattn_W_kr, L0_xattn_Wo, L0_ffn_gate_w, L0_ffn_gu_w, L0_ffn_dp_w,
                                L0_ffn_sh_gate_w, L0_ffn_sh_up_w, L0_ffn_sh_down_w, L0_ffn_sh_gate1_w)]
    f32 = np.float32

    freq = f32(1.0) / f32(10000.0) ** (np.arange(0, DC, 2, dtype=f32) / f32(DC))
    angle = np.arange(L, dtype=f32)[:, None] * freq[None, :]
    cos = np.repeat(np.cos(angle), 2, axis=-1)
    sin = np.repeat(np.sin(angle), 2, axis=-1)
    sin = np.concatenate([-sin[:, :DC // 2], sin[:, DC // 2:]], axis=-1)
    rows = lambda a: a.reshape(NL, P, DC).transpose(1, 0, 2).reshape(P, NL * DC)
    consts = np.concatenate([np.eye(P, dtype=f32), rows(cos), rows(sin),
                             np.concatenate([np.eye(E, dtype=f32)] * 2)], axis=1).astype(f32)

    x_in = x.reshape(NT, P, DIM).transpose(1, 0, 2)
    ctx_in = ctx_512.reshape(B, NL, P, DC).transpose(2, 0, 1, 3)
    gains = np.broadcast_to(np.concatenate([g_xattn, g_ffn])[None, :], (P, 2))
    fq = np.concatenate([Wqr, kcq.transpose(0, 2, 1)], axis=2)
    fq = fq.reshape(HP, 2, 2, QH, R + HK).transpose(0, 3, 1, 2, 4).reshape(HP, QH, W1COLS)
    by_pair = lambda a: a.reshape(HP, 2, HK, -1).transpose(0, 2, 1, 3).reshape(HP, HK, -1)
    fa = np.concatenate([Wkr.transpose(0, 2, 1).reshape(HP, P, DC), by_pair(Wq.reshape(H, HK, DIM))], axis=2)
    fb = by_pair(np.concatenate([kckv, Wo.T.reshape(H, HK, DIM)], axis=2))
    by_chunk = lambda a: a.T.reshape(NC, P, -1).transpose(1, 0, 2)
    gate_in = by_chunk(gate)
    g1_in = np.broadcast_to(by_chunk(shg1), (P, NC, P))
    gu_sh = np.zeros((2, 2, EI, DIM), f32)
    gu_sh[0, 0], gu_sh[1, 0] = shg, shu
    gu_all = gu.reshape(EP, 2, 2, EI, DIM).transpose(0, 2, 1, 3, 4)
    gu_all = np.concatenate([gu_sh[None], gu_all]).reshape(NP, 2, P, NC, P).transpose(0, 4, 3, 1, 2)
    dp_sh = np.zeros((2, EI, DIM), f32)
    dp_sh[0] = shd.T
    dp_all = np.concatenate([dp_sh[None], dp.transpose(0, 2, 1).reshape(EP, 2, EI, DIM)]).reshape(NP, P, DIM)
    experts = np.concatenate([gu_all.reshape(NP, P, GU), dp_all], axis=2)

    arrays = {"x": x_in, "ctx": ctx_in, "consts": consts, "gains": gains, "w_fold_r": fq, "w_fold_a": fa, "w_fold_b": fb,
              "gate_w": gate_in, "shared_gate1": g1_in, "w_experts": experts}
    nc = bacc.Bacc("TRN2", target_bir_lowering=False, num_devices=1)
    ins, args = {}, []
    for name, a in arrays.items():
        a = np.ascontiguousarray(a)
        ins[f"in_{name}"] = a
        args.append(nc.dram_tensor(f"in_{name}", a.shape, mybir.dt.from_np(a.dtype), kind="ExternalInput").ap())
    out = nc.dram_tensor("result", (TOK, DIM), F32, kind="ExternalOutput").ap()
    gated_cross_attention_moe(nc, *args, out.rearrange("(t p) c -> p t c", p=P))
    r = run_bass_kernel_spmd(nc, [ins], core_ids=[0])
    return r.results[0]["result"].reshape(B, S, DIM)
```

```python
from contextlib import ExitStack

import concourse.bass as bass
from concourse import mybir
from concourse.alu_op_type import AluOpType as ALU

F32 = mybir.dt.float32
F32R = mybir.dt.float32r
ACT = mybir.ActivationFunctionType
AX = mybir.AxisListType.X

P = 128
B, S, DIM = 2, 256, 256
L, DC = 512, 64
H, HK, CQ, R = 16, 128, 192, 64
E, EI, TOPK = 64, 64, 8
LN_EPS = 1e-5

TOK = B * S
NT = TOK // P
NC = DIM // P
NS = S // P
NL = L // P
HP = H // 2
QH = CQ // 2
TILES = B * 2 * NS
EP = E // 2
NP = EP + 1
W1COLS = 2 * 2 * (R + HK)
W2COLS = DC + 2 * DIM
W3COLS = 2 * (DC + DIM)
GU = NC * 2 * P
FW = GU + DIM
RING = 4
CI, CC, CS, CZ = 0, P, P + NL * DC, P + 2 * NL * DC
CONSTS = CZ + E
TAKEN = -3.0e38


def gated_cross_attention_moe(nc, x, ctx, consts, gains, w_fold_r, w_fold_a, w_fold_b, gate_w, shared_gate1,
                              w_experts, routed, out):
    with ExitStack() as stack:
        def sb(name, shape, dt=F32):
            return stack.enter_context(nc.sbuf_tensor(name, shape, dt))

        def sem(name):
            return stack.enter_context(nc.semaphore(name))

        bank = [stack.enter_context(nc.psum_tensor(f"bank{i}", [P, 512], F32)) for i in range(8)]

        x_sb = sb("x_sb", [P, NT, DIM])
        ctx_sb = sb("ctx_sb", [P, B, NL, DC])
        con = sb("con", [P, CONSTS])
        gain_raw = sb("gain_raw", [P, 2])
        gain = sb("gain", [P, 2])
        eps = sb("eps", [P, 1])
        gate_raw = sb("gate_raw", [P, NC, E])
        gate_hl = sb("gate_hl", [P, NC, 2, E], F32R)
        g1 = sb("g1", [P, DIM])

        stats = sb("stats", [P, NT, 6])
        meanvar = sb("meanvar", [P, NT, 2])
        stdev = sb("stdev", [P, NT])
        rstd = sb("rstd", [P, NT])
        normed = sb("normed", [P, NT, DIM])
        nT_hi = sb("nT_hi", [P, NC, TOK], F32R)
        nT_lo = sb("nT_lo", [P, NC, TOK], F32R)

        kv = sb("kv", [P, B * NL, 2, DC])
        rot = sb("rot", [P, B * NL, DC])
        turned = sb("turned", [P, B * NL, DC])
        K_hi = sb("K_hi", [P, B, L], F32R)
        K_lo = sb("K_lo", [P, B, L], F32R)

        raw_r = sb("raw_r", [QH, W1COLS])
        raw_a = sb("raw_a", [P, W2COLS])
        raw_b = sb("raw_b", [P, W3COLS])
        rT = sb("rT", [P, HK])
        foldF = sb("foldF", [P, 2, DC])
        A_hi = sb("A_hi", [P, NC, P], F32R)
        A_lo = sb("A_lo", [P, NC, P], F32R)
        Bout_hi = sb("Bout_hi", [P, HP, DIM], F32R)
        Bout_lo = sb("Bout_lo", [P, HP, DIM], F32R)
        Q = [sb(f"Q{h}", [P, TOK], F32R) for h in range(2)]
        nmax = sb("nmax", [P, TILES])
        rsum = sb("rsum", [P, TILES])
        rinv = sb("rinv", [P, TILES])
        prob = [sb(f"prob{i}", [P, L]) for i in range(4)]
        probT = [[sb(f"probT{b}{h}", [P, NL, S]) for h in range(2)] for b in range(B)]
        ctxT_hi = sb("ctxT_hi", [P, HP, TOK], F32R)
        ctxT_lo = sb("ctxT_lo", [P, HP, TOK], F32R)

        x1 = sb("x1", [P, NT, DIM])
        logitT = sb("logitT", [P, TOK])
        logit = sb("logit", [P, NT, E])
        top8 = sb("top8", [P, NT, TOPK])
        cut = sb("cut", [P, NT, E])
        shifted = sb("shifted", [P, NT, E])
        expl = sb("expl", [P, NT, E])
        picked = sb("picked", [P, NT, E])
        psumw = sb("psumw", [P, NT])
        pinv = sb("pinv", [P, NT])
        route = sb("route", [P, NT, E])
        routeT = sb("routeT", [P, TOK], F32R)
        routeT_full = sb("routeT_full", [E, TOK])

        ffn_raw = [sb(f"ffn_raw{i}", [P, FW]) for i in range(RING)]
        ffn_hi = [sb(f"ffn_hi{i}", [P, FW], F32R) for i in range(RING)]
        ffn_lo = [sb(f"ffn_lo{i}", [P, FW], F32R) for i in range(RING)]
        pick = [sb(f"pick{i}", [P, P], F32R) for i in range(3)]
        g1_prod = sb("g1_prod", [P, NT, DIM])
        shared_z = sb("shared_z", [P, NT])
        shared_e = sb("shared_e", [P, NT])
        shared_d = sb("shared_d", [P, NT])
        shared_g = sb("shared_g", [P, NT])
        flat = [probT[b][h][:, :, :].rearrange("p l n -> p (l n)") for b in range(B) for h in range(2)]
        w_rows = [flat[i][:, 0:TOK] for i in range(RING)]
        act_g = [flat[i][:, TOK:2 * TOK] for i in range(2)]
        gu = [flat[2 + i][:, TOK:2 * TOK] for i in range(2)]
        weighted = [prob[i] for i in range(2)]
        in_hi = [sb(f"in_hi{i}", [P, TOK], F32R) for i in range(2)]
        in_lo = [sb(f"in_lo{i}", [P, TOK], F32R) for i in range(2)]
        outT = sb("outT", [P, NC, TOK])
        fin = sb("fin", [P, NT, DIM])

        ident = con[:, CI:CI + P]
        cos = con[:, CC:CC + NL * DC].rearrange("p (l d) -> p l d", l=NL)
        sin = con[:, CS:CS + NL * DC].rearrange("p (l d) -> p l d", l=NL)
        stacked = con[:, CZ:CZ + E]
        out_bank, t_bank = (5, 6, 7, 5), (0, 1, 6, 7)
        tail_gate_bank, tail_up_bank = (0, 4), (2, 5)
        key_bank = (0, 4)
        ln2_groups = (range(0, NS), range(NS, NS + 1), range(NS + 1, NT))

        names = """ctx_loaded con_loaded raw_r_loaded raw_a_loaded raw_b_loaded small_loaded out_stored
            stat1 mv1 sd1 rstd1 norm1 xT1 xhi1 xlo1
            rope_part rope_done kT_made k_hi k_lo
            rT_made rT_copied F_made F_copied A_made A_hi_made A_lo_made B_made B_hi B_lo
            q_made q_hi q_lo scored max_made exp_made inv_made normalised transposed probT_copied
            attended ctx_hi ctx_lo gain_done
            out_made x1_made stat2 mv2 sd2 rstd2 norm2 xT2 xhi2 xlo2
            gate_hi gate_lo logitT_made logitT_copied z_made shared_e_made shared_d_made shared_g_made
            logits_made logits_copied top_made cut_made shift_made expl_made
            picked_made pinv_made route_made routeT_made routeT_hi routeT_lo routeT_full_made routed_stored
            w_hi w_lo pick_made gate_mm up_mm weight_mm silu_made gu_made weighted_made in_hi_made
            in_ready down_mm outT_copied outT_t fin_made
            tail_gate tail_up tail_silu tail_gu tail_weighted tail_hi tail_ready tail_down""".split()
        s = {n: sem(n) for n in names}
        x_loaded = [sem(f"x_loaded{b}") for b in range(B)]
        w_rows_loaded = [sem(f"w_rows_loaded{i}") for i in range(RING)]
        ffn_loaded = [sem(f"ffn_loaded{i}") for i in range(RING)]

        block = stack.enter_context(nc.Block())

        wr_r = w_fold_r.rearrange("t p n -> p t n")
        wa_r = w_fold_a.rearrange("t p n -> p t n")
        wb_r = w_fold_b.rearrange("t p n -> p t n")
        wf_r = w_experts.rearrange("t p n -> p t n")

        def tile_of(i):
            return i // (2 * NS), i // NS % 2, i % NS

        def dyn(ap3, t):
            return ap3[:, bass.ds(t, 1), :].rearrange("p a n -> p (a n)")

        @block.sync
        def _(sp):
            def load_r(t):
                sp.dma_start(raw_r[:, :], dyn(wr_r, t)).then_inc(s["raw_r_loaded"], 16)

            def load_a(t):
                sp.dma_start(raw_a[:, :], dyn(wa_r, t)).then_inc(s["raw_a_loaded"], 16)

            def load_b(t):
                sp.dma_start(raw_b[:, :], dyn(wb_r, t)).then_inc(s["raw_b_loaded"], 16)

            load_r(0)
            load_a(0)
            for b in range(B):
                rows = slice(b * NS, (b + 1) * NS)
                sp.dma_start(x_sb[:, rows, :], x[:, rows, :]).then_inc(x_loaded[b], 16)
            sp.dma_start(con[:, :], consts).then_inc(s["con_loaded"], 16)
            sp.dma_start(ctx_sb[:, :, :, :], ctx).then_inc(s["ctx_loaded"], 16)
            load_b(0)
            sp.dma_start(gain_raw[:, :], gains).then_inc(s["small_loaded"], 16)
            sp.dma_start(gate_raw[:, :, :], gate_w).then_inc(s["small_loaded"], 16)
            sp.dma_start(g1[:, :], shared_gate1).then_inc(s["small_loaded"], 16)
            for q in range(RING):
                sp.dma_start(ffn_raw[q][:, :], dyn(wf_r, q)).then_inc(ffn_loaded[q], 16)
            with sp.Fori(1, HP) as t:
                sp.wait_ge(s["rT_made"], t)
                load_r(t)
                sp.wait_ge(s["A_made"], t)
                load_a(t)
                sp.wait_ge(s["B_made"], t)
                load_b(t)

            def load_ffn(slot, q):
                sp.wait_ge(s["w_lo"], q - RING + 1)
                sp.dma_start(ffn_raw[slot][:, :], dyn(wf_r, q)).then_inc(ffn_loaded[slot], 16)

            def load_w_rows(slot, q, free=True):
                if free:
                    sp.wait_ge(s["weighted_made"], q - RING + 1)
                for e in range(2):
                    sp.dma_start(w_rows[slot][e * EI:(e + 1) * EI, :],
                                 routed[bass.ds((q - 1) * 2 + e, 1), :].to_broadcast([EI, TOK]))\
                        .then_inc(w_rows_loaded[slot], 16)

            for q in range(RING, 2 * RING):
                load_ffn(q % RING, q)
            sp.wait_ge(s["routeT_full_made"], 1)
            sp.dma_start(routed, routeT_full[:, :]).then_inc(s["routed_stored"], 16)
            sp.wait_ge(s["routed_stored"], 16)
            for q in range(3, RING + 3):
                load_w_rows(q % RING, q, free=False)
            for q in range(2 * RING, 2 * RING + 2):
                load_ffn(q % RING, q)
                load_w_rows((q - 1) % RING, q - 1)
            looped = (NP - 2 * RING - 2) // RING
            with sp.Fori(0, looped) as u:
                for j in range(RING):
                    load_ffn((j + 2) % RING, u * RING + j + 2 * RING + 2)
                    load_w_rows((j + 1) % RING, u * RING + j + 2 * RING + 1)
            for q in range((looped + 2) * RING + 2, NP):
                load_ffn(q % RING, q)
                load_w_rows((q - 1) % RING, q - 1)
            load_w_rows((NP - 1) % RING, NP - 1)
            for tt in range(NT):
                sp.wait_ge(s["fin_made"], tt + 1)
                sp.dma_start(out[:, tt, :], fin[:, tt, :]).then_inc(s["out_stored"], 16)
            sp.wait_ge(s["out_stored"], 16 * NT)

        @block.gpsimd
        def _(pool):
            def split_lo(slot, q):
                pool.wait_ge(s["w_hi"], q + 1)
                nc.gpsimd.tensor_tensor(ffn_lo[slot][:, :], ffn_raw[slot][:, :], ffn_hi[slot][:, :].bitcast(F32),
                                        ALU.subtract).then_inc(s["w_lo"], 1)

            half = DC // 2
            add, mult, combine = ALU.add, ALU.mult, nc.gpsimd.tensor_tensor
            pool.wait_ge(s["con_loaded"], 16)
            pool.wait_ge(s["ctx_loaded"], 16)
            for b in range(B):
                rows = slice(b * NL, (b + 1) * NL)
                combine(rot[:, rows, 0:half], ctx_sb[:, b, :, half:DC], sin[:, :, 0:half],
                        mult).then_inc(s["rope_part"], 1)
                combine(rot[:, rows, half:DC], ctx_sb[:, b, :, 0:half], sin[:, :, half:DC],
                        mult).then_inc(s["rope_part"], 1)
                combine(turned[:, rows, :], ctx_sb[:, b, :, :], cos, mult).then_inc(s["rope_part"], 1)
                pool.wait_ge(s["rope_part"], 3 * b + 3)
                combine(kv[:, rows, 0, :], turned[:, rows, :], rot[:, rows, :], add).then_inc(s["rope_done"], 1)
                combine(kv[:, rows, 1, :], turned[:, rows, :], rot[:, rows, :], add).then_inc(s["rope_done"], 1)

            pool.wait_ge(s["small_loaded"], 48)
            pool.wait_ge(s["gate_hi"], 1)
            nc.gpsimd.tensor_tensor(gate_hl[:, :, 1, :], gate_raw[:, :, :], gate_hl[:, :, 0, :].bitcast(F32),
                                    ALU.subtract).then_inc(s["gate_lo"], 1)
            for q in range(2):
                split_lo(q, q)
            with pool.Fori(0, (NP - 1) // RING - 1) as u:
                for j in range(RING):
                    split_lo((2 + j) % RING, u * RING + j + 2)
            for q in range(NP - 1 - RING + 2, NP):
                split_lo(q % RING, q)

        @block.scalar
        def _(act):
            def copy(dst, src, done):
                nc.scalar.activation(dst, src, ACT.Copy).then_inc(s[done], 1)

            for b in range(B):
                rows = slice(b * NS, (b + 1) * NS)
                act.wait_ge(s["mv1"], (b + 1) * NS)
                nc.scalar.activation(stdev[:, rows], meanvar[:, rows, 1], ACT.Sqrt,
                                     bias=eps[:, 0:1]).then_inc(s["sd1"], 1)

            act.preload_act_table(ACT.Exp)

            def fold_hi(t):
                act.wait_ge(s["A_made"], t + 1)
                copy(A_hi[:, :, :], bank[6][:, 0:NC * P].rearrange("p (c n) -> p c n", c=NC), "A_hi_made")

            def split_nT_hi(tt, b, made, done):
                act.wait_ge(s[made], tt + 1)
                copy(nT_hi[:, :, tt * P:(tt + 1) * P], bank[b][:, 0:NC * P].rearrange("p (c n) -> p c n", c=NC), done)

            def K_split_hi(b):
                act.wait_ge(s["kT_made"], b + 1)
                copy(K_hi[:, b, :], bank[key_bank[b]][:, :], "k_hi")

            def q_hi(t, h):
                act.wait_ge(s["q_made"], t + 1)
                copy(Q[h][0:DC, :], bank[5][DC * h:DC * h + DC, :], "q_hi")

            def copy_B(t):
                act.wait_ge(s["B_made"], t + 1)
                copy(dyn(Bout_hi, t), bank[7][:, DIM:2 * DIM], "B_hi")

            fold_hi(0)
            for tt in range(NT):
                split_nT_hi(tt, 1 + tt, "xT1", "xhi1")
            K_split_hi(0)
            q_hi(0, 0)
            copy_B(0)

            def exponentials(t, i):
                act.wait_ge(s["max_made"], t * TILES + i + 1)
                nc.scalar.activation(prob[i % 4][:, :], bank[i % 2][:, :], ACT.Exp, bias=nmax[:, i:i + 1],
                                     accum_out=rsum[:, i:i + 1]).then_inc(s["exp_made"], 1)

            def copy_probT(t, i):
                b, h, sc = tile_of(i)
                act.wait_ge(s["transposed"], t * TILES + i + 1)
                copy(probT[b][h][:, :, sc * P:(sc + 1) * P], bank[2 + i % 2][:, :].rearrange("p (l n) -> p l n", l=NL),
                     "probT_copied")

            def copy_ctx(t, b):
                act.wait_ge(s["attended"], t * B + b + 1)
                copy(dyn(ctxT_hi[:, :, b * S:(b + 1) * S], t), bank[4][:, 0:S], "ctx_hi")

            def first_weights_hi(q):
                act.wait_ge(ffn_loaded[q], 16)
                copy(ffn_hi[q][:, :], ffn_raw[q][:, :], "w_hi")

            def make_pick(slot, q):
                src = stacked[:, bass.ds((q - 1) * 2, 2)]
                nc.scalar.activation(pick[slot][:, :].rearrange("p (e n) -> p e n", e=2),
                                     src.unsqueeze(2).to_broadcast([P, 2, EI]), ACT.Copy).then_inc(s["pick_made"], 1)

            def pair(t, first, last):
                for i in range(TILES):
                    if i == 0:
                        q_hi(t, 1)
                    if first and i == 1:
                        K_split_hi(1)
                    if first and i == 3:
                        act.wait_ge(s["small_loaded"], 48)
                        copy(gate_hl[:, :, 0, :], gate_raw[:, :, :], "gate_hi")
                        nc.scalar.activation(gain[:, :], gain_raw[:, :], ACT.Tanh).then_inc(s["gain_done"], 1)
                    if not first and i in (1, 5):
                        copy_ctx(t - 1, i // 4)
                    if i == 6 and not last:
                        q_hi(t + 1, 0)
                    exponentials(t, i)
                    if i >= 2:
                        copy_probT(t, i - 2)
                    elif not first:
                        copy_probT(t - 1, TILES + i - 2)
                    if last and i in (2, 4, 6):
                        first_weights_hi(i // 2 - 1)
                    if last and i in (3, 5):
                        make_pick(i // 2, i // 2)
                    if not last:
                        if i == 2:
                            copy_B(t + 1)
                        if i == 3:
                            fold_hi(t + 1)

            pair(0, True, False)
            with act.Fori(1, HP - 1) as t:
                pair(t, False, False)
            pair(HP - 1, False, True)
            copy_ctx(HP - 1, 0)
            copy_probT(HP - 1, TILES - 2)
            copy_probT(HP - 1, TILES - 1)
            act.preload_act_table(ACT.Sqrt)

            def copy_logitT(b):
                cols = slice(b * S, (b + 1) * S)
                act.wait_ge(s["logitT_made"], b + 1)
                copy(logitT[:, cols], bank[4][:, cols], "logitT_copied")

            for g, tiles in enumerate(ln2_groups):
                rows = slice(tiles[0], tiles[-1] + 1)
                act.wait_ge(s["mv2"], tiles[-1] + 1)
                nc.scalar.activation(stdev[:, rows], meanvar[:, rows, 1], ACT.Sqrt,
                                     bias=eps[:, 0:1]).then_inc(s["sd2"], 1)
                if g == 0:
                    for tt in tiles:
                        split_nT_hi(tt, t_bank[tt], "xT2", "xhi2")
                    copy_ctx(HP - 1, 1)
                    first_weights_hi(3)
                if g == 1:
                    copy_logitT(0)
            for tt in range(NS, NT):
                split_nT_hi(tt, t_bank[tt], "xT2", "xhi2")
            copy_logitT(1)
            act.preload_act_table(ACT.Exp)
            act.wait_ge(s["z_made"], NT)
            nc.scalar.activation(shared_e[:, :], shared_z[:, :], ACT.Exp, scale=-1.0).then_inc(s["shared_e_made"], 1)
            act.wait_ge(s["shift_made"], B)
            nc.scalar.activation(expl[:, :, :], shifted[:, :, :], ACT.Exp).then_inc(s["expl_made"], 1)
            act.preload_act_table(ACT.Silu)

            def silu(j, q, first=False):
                act.wait_ge(s["gate_mm"], q + 1)
                if not first:
                    act.wait_ge(s["gu_made"], q - 1)
                nc.scalar.activation(act_g[j % 2][:, :], bank[j % 2][:, :], ACT.Silu).then_inc(s["silu_made"], 1)

            silu(0, 0, first=True)
            act.wait_ge(s["routeT_made"], 1)
            copy(routeT[0:E, :], bank[7][0:E, :], "routeT_hi")

            def step(j, q, ahead=True):
                silu(j, q)
                if ahead:
                    act.wait_ge(s["down_mm"], q - 1)
                    slot = (j + 2) % RING
                    act.wait_ge(ffn_loaded[slot], ((j + 2) // RING) * 16 + (q - j) * (16 // RING) + 16)
                    copy(ffn_hi[slot][:, :], ffn_raw[slot][:, :], "w_hi")

            silu(1, 1, first=True)
            act.wait_ge(s["routeT_lo"], 1)
            copy(routeT_full[:, :], bank[7][0:E, :], "routeT_full_made")
            for j in range(2, RING):
                step(j, j)
            step(RING, RING)
            with act.Fori(1, (NP - 1) // RING - 1) as u:
                for j in range(1, RING + 1):
                    step(j, u * RING + j)
            for q in range(NP - RING, NP - 1):
                step(q, q, ahead=q + 2 < NP)
            act.wait_ge(s["gu_made"], NP - 2)
            for b in range(B):
                cols = slice(b * S, (b + 1) * S)
                act.wait_ge(s["tail_gate"], b + 1)
                nc.scalar.activation(act_g[(NP - 1) % 2][:, cols], bank[tail_gate_bank[b]][:, cols],
                                     ACT.Silu).then_inc(s["tail_silu"], 1)

            for b in range(B):
                cols = slice(b * S, (b + 1) * S)
                act.wait_ge(s["tail_down"], b + 1)
                for c in range(NC):
                    copy(outT[:, c, cols], bank[6 + c][:, cols], "outT_copied")

        @block.vector
        def _(dve):
            v = nc.vector

            def hold(name, n):
                dve.wait_ge(s[name], n)

            v.memset(eps[:, :], LN_EPS)

            def copy_rT(t):
                hold("rT_made", t + 1)
                v.tensor_copy(rT[:, :], bank[6][:, 0:HK]).then_inc(s["rT_copied"], 1)

            def copy_F(t):
                hold("F_made", t + 1)
                v.tensor_copy(foldF[:, 0, :], bank[6][:, 0:DC]).then_inc(s["F_copied"], 1)
                v.tensor_copy(foldF[:, 1, :], bank[7][:, 0:DC]).then_inc(s["F_copied"], 1)

            def B_split_lo(t):
                hold("B_hi", t + 1)
                v.tensor_tensor(dyn(Bout_lo, t), bank[7][:, DIM:2 * DIM], dyn(Bout_hi, t).bitcast(F32),
                                ALU.subtract).then_inc(s["B_lo"], 1)

            def ctx_split_lo(t, b):
                hold("ctx_hi", t * B + b + 1)
                v.tensor_tensor(dyn(ctxT_lo[:, :, b * S:(b + 1) * S], t), bank[4][:, 0:S],
                                dyn(ctxT_hi[:, :, b * S:(b + 1) * S], t).bitcast(F32),
                                ALU.subtract).then_inc(s["ctx_lo"], 1)

            def fold_lo(t):
                hold("A_hi_made", t + 1)
                v.tensor_tensor(A_lo[:, :, :], bank[6][:, 0:NC * P].rearrange("p (c n) -> p c n", c=NC),
                                A_hi[:, :, :].bitcast(F32), ALU.subtract).then_inc(s["A_lo_made"], 1)

            def q_lo(t, h):
                hold("q_hi", 2 * t + h + 1)
                v.tensor_tensor(Q[h][DC:P, :], bank[5][DC * h:DC * h + DC, :], Q[h][0:DC, :].bitcast(F32),
                                ALU.subtract).then_inc(s["q_lo"], 1)

            def split_nT_lo(tt, b, hi, done):
                hold(hi, tt + 1)
                v.tensor_tensor(nT_lo[:, :, tt * P:(tt + 1) * P],
                                bank[b][:, 0:NC * P].rearrange("p (c n) -> p c n", c=NC),
                                nT_hi[:, :, tt * P:(tt + 1) * P].bitcast(F32), ALU.subtract).then_inc(s[done], 1)

            def K_split_lo(b):
                hold("k_hi", b + 1)
                v.tensor_tensor(K_lo[:, b, :], bank[key_bank[b]][:, :], K_hi[:, b, :].bitcast(F32),
                                ALU.subtract).then_inc(s["k_lo"], 1)

            def variances(src, tiles, k):
                for tt in tiles:
                    v.bn_stats(stats[:, tt, :], src[:, tt, :]).then_inc(s[f"stat{k}"], 1)
                for tt in tiles:
                    hold(f"stat{k}", tt + 1)
                    v.bn_aggr(meanvar[:, tt, :], stats[:, tt, :]).then_inc(s[f"mv{k}"], 1)

            def normed_rows(src, g, tiles, k):
                rows = slice(tiles[0], tiles[-1] + 1)
                hold(f"sd{k}", g + 1)
                v.reciprocal(rstd[:, rows], stdev[:, rows]).then_inc(s[f"rstd{k}"], 1)
                hold(f"rstd{k}", g + 1)
                for tt in tiles:
                    v.tensor_scalar(normed[:, tt, :], src[:, tt, :], meanvar[:, tt, 0:1], rstd[:, tt:tt + 1],
                                    ALU.subtract, ALU.mult).then_inc(s[f"norm{k}"], 1)

            copy_rT(0)
            dve.wait_ge(x_loaded[0], 16)
            variances(x_sb, range(0, NS), 1)
            copy_F(0)
            dve.wait_ge(x_loaded[1], 16)
            variances(x_sb, range(NS, NT), 1)
            normed_rows(x_sb, 0, range(0, NS), 1)
            normed_rows(x_sb, 1, range(NS, NT), 1)
            for tt in range(NT):
                split_nT_lo(tt, 1 + tt, "xhi1", "xlo1")
                if tt == 1:
                    fold_lo(0)
            K_split_lo(0)
            q_lo(0, 0)
            B_split_lo(0)

            def row_max(t, i):
                hold("scored", t * TILES + i + 1)
                v.tensor_reduce(nmax[:, i:i + 1], bank[i % 2][:, :], AX, ALU.max,
                                negate=True).then_inc(s["max_made"], 1)

            def invert(t, i):
                hold("exp_made", t * TILES + i + 1)
                v.reciprocal(rinv[:, i:i + 1], rsum[:, i:i + 1]).then_inc(s["inv_made"], 1)

            def normalise(t, i):
                hold("inv_made", t * TILES + i + 1)
                v.tensor_scalar(prob[i % 4][:, :], prob[i % 4][:, :], rinv[:, i:i + 1], None,
                                ALU.mult).then_inc(s["normalised"], 1)

            def pair(t, first, last):
                for i in range(TILES):
                    early = i == 0
                    if not early:
                        row_max(t, i)
                    if i:
                        normalise(t, i - 1)
                    elif not first:
                        normalise(t - 1, TILES - 1)
                    if early:
                        row_max(t, i)
                    if i == 0:
                        q_lo(t, 1)
                    if first and i == 1:
                        K_split_lo(1)
                    if not first and i in (2, 5):
                        ctx_split_lo(t - 1, i // 4)
                    if not last:
                        if i == 0:
                            copy_rT(t + 1)
                        if i == 1:
                            copy_F(t + 1)
                        if i == 3:
                            B_split_lo(t + 1)
                        if i == 4:
                            fold_lo(t + 1)
                        if i == 6:
                            q_lo(t + 1, 0)
                    invert(t, i)

            pair(0, True, False)
            with dve.Fori(1, HP - 1) as t:
                pair(t, False, False)
            pair(HP - 1, False, True)
            ctx_split_lo(HP - 1, 0)
            normalise(HP - 1, TILES - 1)

            hold("gain_done", 1)

            def shared_logit(tt):
                hold("norm2", tt + 1)
                v.scalar_tensor_tensor(out=g1_prod[:, tt, :], in0=normed[:, tt, :], scalar=1.0, in1=g1[:, :],
                                       op0=ALU.mult, op1=ALU.mult,
                                       accum_out=shared_z[:, tt:tt + 1]).then_inc(s["z_made"], 1)

            def residual(tiles):
                for tt in tiles:
                    hold("out_made", tt + 1)
                    v.scalar_tensor_tensor(out=x1[:, tt, :], in0=bank[out_bank[tt]][:, 0:DIM], scalar=gain[:, 0:1],
                                           in1=x_sb[:, tt, :], op0=ALU.mult, op1=ALU.add).then_inc(s["x1_made"], 1)
                hold("x1_made", tiles[-1] + 1)
                variances(x1, tiles, 2)

            residual(ln2_groups[0])
            normed_rows(x1, 0, ln2_groups[0], 2)
            for tt in ln2_groups[0]:
                shared_logit(tt)
            for tt in ln2_groups[0]:
                split_nT_lo(tt, t_bank[tt], "xhi2", "xlo2")
            ctx_split_lo(HP - 1, 1)
            residual(ln2_groups[1])
            residual(ln2_groups[2])
            normed_rows(x1, 1, ln2_groups[1], 2)
            normed_rows(x1, 2, ln2_groups[2], 2)
            split_nT_lo(NT - 2, t_bank[NT - 2], "xhi2", "xlo2")
            for tt in (NT - 2, NT - 1):
                shared_logit(tt)
            split_nT_lo(NT - 1, t_bank[NT - 1], "xhi2", "xlo2")

            for b in range(B):
                tiles = range(b * NS, (b + 1) * NS)
                rows = slice(b * NS, (b + 1) * NS)
                hold("logits_made", b + 1)
                v.tensor_copy(logit[:, rows, :],
                              bank[5][:, b * NS * E:(b + 1) * NS * E].rearrange("p (t e) -> p t e", t=NS)
                              ).then_inc(s["logits_copied"], 1)
                hold("logits_copied", b + 1)
                for tt in tiles:
                    v.max(top8[:, tt, :], logit[:, tt, :]).then_inc(s["top_made"], 1)
                hold("top_made", (b + 1) * NS)
                v.tensor_tensor(shifted[:, rows, :], logit[:, rows, :], top8[:, rows, 0:1].to_broadcast([P, NS, E]),
                                ALU.subtract).then_inc(s["shift_made"], 1)
                for tt in tiles:
                    v.match_replace(cut[:, tt, :], top8[:, tt, :], logit[:, tt, :], TAKEN).then_inc(s["cut_made"], 1)
            hold("shared_e_made", 1)
            v.tensor_scalar(shared_d[:, :], shared_e[:, :], 1.0, None, ALU.add).then_inc(s["shared_d_made"], 1)
            hold("shared_d_made", 1)
            v.reciprocal(shared_g[:, :], shared_d[:, :]).then_inc(s["shared_g_made"], 1)
            hold("cut_made", NT)
            hold("expl_made", 1)
            for tt in range(NT):
                v.scalar_tensor_tensor(out=picked[:, tt, :], in0=cut[:, tt, :], scalar=TAKEN, in1=expl[:, tt, :],
                                       op0=ALU.is_equal, op1=ALU.mult,
                                       accum_out=psumw[:, tt:tt + 1]).then_inc(s["picked_made"], 1)
            hold("picked_made", NT)
            v.reciprocal(pinv[:, :], psumw[:, :]).then_inc(s["pinv_made"], 1)
            hold("pinv_made", 1)
            v.tensor_tensor(route[:, :, :], picked[:, :, :], pinv[:, :].unsqueeze(2).to_broadcast([P, NT, E]),
                            ALU.mult).then_inc(s["route_made"], 1)

            def inner(j, q, first=False, shared=False, loads=None):
                hold("silu_made", q + 1)
                hold("up_mm", q + 1)
                v.tensor_tensor(gu[j % 2][:, :], act_g[j % 2][:, :], bank[2 + j % 2][:, :],
                                ALU.mult).then_inc(s["gu_made"], 1)
                hold("gu_made", q + 1)
                if shared:
                    hold("routeT_hi", 1)
                    v.tensor_tensor(routeT[E:2 * E, :], bank[7][0:E, :], routeT[0:E, :].bitcast(F32),
                                    ALU.subtract).then_inc(s["routeT_lo"], 1)
                if loads is None:
                    hold("weight_mm", q + 1)
                    w = bank[4 + j % 2]
                else:
                    dve.wait_ge(w_rows_loaded[j % RING], 32 * loads)
                    w = w_rows[j % RING]
                v.tensor_tensor(weighted[j % 2][:, :], gu[j % 2][:, :], w[:, :],
                                ALU.mult).then_inc(s["weighted_made"], 1)
                if not first:
                    hold("down_mm", q - 1)
                hold("weighted_made", q + 1)
                v.tensor_copy(in_hi[j % 2][:, :], weighted[j % 2][:, :]).then_inc(s["in_hi_made"], 1)
                hold("in_hi_made", q + 1)
                v.tensor_tensor(in_lo[j % 2][:, :], weighted[j % 2][:, :], in_hi[j % 2][:, :].bitcast(F32),
                                ALU.subtract).then_inc(s["in_ready"], 1)

            inner(0, 0, first=True, shared=True)
            inner(1, 1, first=True)
            inner(2, 2)
            for q in range(3, RING + 1):
                inner(q, q, loads=1)

            def loads_more(j):
                return j // 3

            with dve.Fori(1, (NP - 1) // RING - 1) as u:
                for j in range(1, RING + 1):
                    inner(j, u * RING + j, loads=u + loads_more(j))
            for j in range(1, RING):
                inner(j, NP - 1 - RING + j, loads=(NP - 1) // RING - 1 + loads_more(j))

            q = NP - 1
            last = q % 2
            hold("down_mm", q - 1)
            dve.wait_ge(w_rows_loaded[q % RING], 32 * ((NP - 1) // RING))
            for b in range(B):
                cols = slice(b * S, (b + 1) * S)
                hold("tail_silu", b + 1)
                hold("tail_up", b + 1)
                v.tensor_tensor(gu[last][:, cols], act_g[last][:, cols], bank[tail_up_bank[b]][:, cols],
                                ALU.mult).then_inc(s["tail_gu"], 1)
                hold("tail_gu", b + 1)
                v.tensor_tensor(weighted[last][:, cols], gu[last][:, cols], w_rows[q % RING][:, cols],
                                ALU.mult).then_inc(s["tail_weighted"], 1)
                hold("tail_weighted", b + 1)
                v.tensor_copy(in_hi[last][:, cols], weighted[last][:, cols]).then_inc(s["tail_hi"], 1)
                hold("tail_hi", b + 1)
                v.tensor_tensor(in_lo[last][:, cols], weighted[last][:, cols], in_hi[last][:, cols].bitcast(F32),
                                ALU.subtract).then_inc(s["tail_ready"], 1)
            for tt in range(NT):
                hold("outT_t", tt + 1)
                v.scalar_tensor_tensor(out=fin[:, tt, :], in0=bank[tt][:, 0:DIM], scalar=gain[:, 1:2],
                                       in1=x1[:, tt, :], op0=ALU.mult, op1=ALU.add).then_inc(s["fin_made"], 1)

        @block.tensor
        def _(pe):
            mm = nc.tensor.matmul

            def hold(name, n):
                pe.wait_ge(s[name], n)

            def fold_r(t):
                hold("raw_r_loaded", t * 16 + 16)
                for c in range(2):
                    for h in range(2):
                        at = (2 * h + c) * (R + HK)
                        last = mm(bank[6][R * h:R * h + R, 0:HK], raw_r[:, at:at + R], raw_r[:, at + R:at + R + HK],
                                  start=(c == 0), stop=(c == 1))
                last.then_inc(s["rT_made"], 1)

            def fold_f(t):
                hold("rT_copied", t + 1)
                hold("raw_a_loaded", t * 16 + 16)
                for h in range(2):
                    last = mm(bank[6 + h][:, 0:DC], rT[R * h:R * h + R, :], raw_a[R * h:R * h + R, 0:DC],
                              start=True, stop=True)
                last.then_inc(s["F_made"], 1)

            def fold_a(t):
                hold("F_copied", 2 * t + 2)
                for h in range(2):
                    for c in range(NC):
                        at = DC + h * DIM + c * P
                        last = mm(bank[6][:, c * P + h * DC:c * P + (h + 1) * DC], raw_a[:, at:at + P],
                                  foldF[:, h, :], start=True, stop=True)
                last.then_inc(s["A_made"], 1)

            def fold_b(t, last_copied=True):
                hold("raw_b_loaded", t * 16 + 16)
                if last_copied:
                    hold("B_lo", t)
                for h in range(2):
                    at = h * (DC + DIM)
                    last = mm(bank[7][DC * h:DC * h + DC, DIM:2 * DIM], raw_b[:, at:at + DC],
                              raw_b[:, at + DC:at + DC + DIM], start=True, stop=True)
                last.then_inc(s["B_made"], 1)

            parts = [(A_hi, nT_hi, c) for c in range(NC)] + [(A_hi, nT_lo, c) for c in range(NC)] \
                + [(A_lo, nT_hi, c) for c in range(NC)]

            def queries(t):
                hold("A_hi_made", t + 1)
                hold("A_lo_made", t + 1)
                for n, (w, y, c) in enumerate(parts):
                    last = mm(bank[5][:, :], w[:, c, :], y[:, c, :], start=(n == 0), stop=(n == len(parts) - 1))
                last.then_inc(s["q_made"], 1)

            def transpose_normed(tt, b, norm, done):
                hold(norm, tt + 1)
                for c in range(NC):
                    last = nc.tensor.transpose(bank[b][:, c * P:(c + 1) * P], normed[:, tt, c * P:(c + 1) * P], ident)
                last.then_inc(s[done], 1)

            def transpose_keys(b):
                hold("rope_done", 2 * b + 2)
                for c in range(NL):
                    last = nc.tensor.transpose(bank[key_bank[b]][:, c * P:(c + 1) * P],
                                               kv[:, b * NL + c, :, :].rearrange("p a d -> p (a d)"), ident)
                last.then_inc(s["kT_made"], 1)

            fold_r(0)
            fold_f(0)
            fold_a(0)
            hold("con_loaded", 16)
            for tt in range(NT):
                transpose_normed(tt, 1 + tt, "norm1", "xT1")
            transpose_keys(0)
            hold("xlo1", NT)
            queries(0)
            fold_b(0, last_copied=False)
            transpose_keys(1)
            hold("k_lo", 1)

            def scores(t, i, first):
                b, h, sc = tile_of(i)
                if first and i == 2 * NS:
                    hold("k_lo", B)
                if b == 0 and sc == 0:
                    hold("q_lo", 2 * t + h + 1)
                rows = slice(b * S + sc * P, b * S + (sc + 1) * P)
                mm(bank[i % 2][:, :], Q[h][:, rows], K_hi[:, b, :], start=True, stop=False)
                mm(bank[i % 2][:, :], Q[h][:, rows], K_lo[:, b, :], start=False, stop=True).then_inc(s["scored"], 1)

            def transposes(t, i, free=True):
                if free:
                    hold("probT_copied", t * TILES + i - 1)
                hold("normalised", t * TILES + i + 1)
                for c in range(NL):
                    last = nc.tensor.transpose(bank[2 + i % 2][:, c * P:(c + 1) * P], prob[i % 4][:, c * P:(c + 1) * P],
                                               ident)
                last.then_inc(s["transposed"], 1)

            def attend(t, b, chunks, free=True):
                if chunks[0] == 0:
                    hold("probT_copied", t * TILES + (b + 1) * 2 * NS)
                    if free:
                        hold("ctx_lo", t * B + b)
                for c in chunks:
                    for h in range(2):
                        last = mm(bank[4][DC * h:DC * h + DC, 0:S], kv[:, b * NL + c, 0, :], probT[b][h][:, c, :],
                                  start=(c == 0), stop=(c == NL - 1))
                if chunks[-1] == NL - 1:
                    last.then_inc(s["attended"], 1)

            first_half, second_half = range(NL // 2), range(NL // 2, NL)

            def project(tt, pairs):
                hold("B_lo", pairs[-1] + 1)
                hold("ctx_lo", pairs[-1] * B + tt // NS + 1)
                if tt == 3:
                    hold("x1_made", 1)
                if tt == 0:
                    hold("q_lo", 2 * HP)
                rows = slice(tt * P, (tt + 1) * P)
                for p in pairs:
                    for n, (y, w) in enumerate(((ctxT_hi, Bout_hi), (ctxT_lo, Bout_hi), (ctxT_hi, Bout_lo))):
                        last = mm(bank[out_bank[tt]][:, 0:DIM], y[:, p, rows], w[:, p, :],
                                  start=(p == 0 and n == 0), stop=(p == HP - 1 and n == 2))
                if p == HP - 1:
                    last.then_inc(s["out_made"], 1)

            def pair(t, first, last):
                for i in range(TILES):
                    if not first or i >= 2:
                        hold("exp_made", t * TILES + i - 1)
                    scores(t, i, first)
                    if not last and i == 0:
                        fold_r(t + 1)
                    if i >= 2:
                        transposes(t, i - 2, free=not first or i >= 4)
                    elif not first:
                        transposes(t - 1, TILES + i - 2)
                    if not last:
                        if i == 1:
                            fold_b(t + 1)
                            fold_f(t + 1)
                        if i == 2:
                            fold_a(t + 1)
                        if i == 5:
                            queries(t + 1)
                    if not first and i in (3, 4):
                        attend(t - 1, 1, (first_half, second_half)[i - 3])
                    if last and i == 1:
                        project(1, (0, 1, 2))
                    if last and i == 2:
                        project(0, (0, 1, 2))
                    if last and i == 5:
                        project(0, (3, 4, 5, 6))
                    if i >= 6:
                        attend(t, 0, (first_half, second_half)[i - 6], free=not first)

            pair(0, True, False)
            with pe.Fori(1, HP - 1) as t:
                pair(t, False, False)
            pair(HP - 1, False, True)

            project(1, (3,))
            transposes(HP - 1, TILES - 2)
            project(1, (4, 5, 6))
            transposes(HP - 1, TILES - 1)
            project(0, (HP - 1,))
            project(1, (HP - 1,))
            project(2, range(HP - 1))
            attend(HP - 1, 1, first_half)
            for tt in range(NS):
                transpose_normed(tt, t_bank[tt], "norm2", "xT2")
            attend(HP - 1, 1, second_half)
            project(3, (0, 1, 2))
            project(2, (HP - 1,))
            project(3, range(3, HP))

            def parts_of(dst, hi, lo, b=None):
                cols = slice(0, TOK) if b is None else slice(b * S, (b + 1) * S)
                n = 0
                for c in range(NC):
                    for w, y in ((hi(c), nT_hi), (hi(c), nT_lo), (lo(c), nT_hi)):
                        last = mm(dst[:, cols], w, y[:, c, cols], start=(n == 0), stop=(n == 3 * NC - 1))
                        n += 1
                return last

            def logits_transposed(b):
                cols = slice(b * S, (b + 1) * S)
                n = 0
                for c in range(NC):
                    for y in (nT_hi, nT_lo):
                        last = mm(bank[4][:, cols], gate_hl[:, c, :, :].rearrange("p a e -> p (a e)"), y[:, c, cols],
                                  start=(n == 0), stop=(n == 2 * NC - 1))
                        n += 1
                last.then_inc(s["logitT_made"], 1)

            def gate_or_up(j, q, k, b=None):
                slot = j % RING
                return parts_of(bank[2 * k + j % 2],
                                lambda c: ffn_hi[slot][:, (2 * c + k) * P:(2 * c + k + 1) * P],
                                lambda c: ffn_lo[slot][:, (2 * c + k) * P:(2 * c + k + 1) * P], b)

            def gate(j, q):
                hold("w_lo", q + 1)
                hold("silu_made", q - 1)
                gate_or_up(j, q, 0).then_inc(s["gate_mm"], 1)

            def up(j, q):
                hold("gu_made", q - 1)
                gate_or_up(j, q, 1).then_inc(s["up_mm"], 1)

            def gate_up(j, q):
                gate(j, q)
                up(j, q)

            def weight(j, q, free=True):
                hold("pick_made", q)
                if free:
                    hold("weighted_made", q - 1)
                mm(bank[4 + j % 2][:, :], pick[j][:, :], routeT[:, :], start=True,
                   stop=True).then_inc(s["weight_mm"], 1)

            def down(j, q, first=False):
                hold("in_ready", q + 1)
                down_parts(j, slice(0, TOK), first).then_inc(s["down_mm"], 1)

            def down_parts(j, cols, first=False, last_pair=False):
                slot = j % RING
                for c in range(NC):
                    rows = slice(GU + c * P, GU + (c + 1) * P)
                    for n, (w, y) in enumerate(((ffn_hi, in_hi), (ffn_hi, in_lo), (ffn_lo, in_hi))):
                        last = mm(bank[6 + c][:, cols], w[slot][:, rows], y[j % 2][:, cols], start=(first and n == 0),
                                  stop=(last_pair and n == 2), skip_group_check=True)
                return last

            def logits_back(b):
                hold("logitT_copied", b + 1)
                if b:
                    hold("logits_copied", b)
                for tt in range(b * NS, (b + 1) * NS):
                    last = mm(bank[5][:, tt * E:(tt + 1) * E], logitT[:, tt * P:(tt + 1) * P], stacked,
                              start=True, stop=True)
                last.then_inc(s["logits_made"], 1)

            hold("gate_lo", 1)
            hold("ctx_lo", HP * B)
            hold("xlo2", NS)
            logits_transposed(0)
            hold("w_lo", 2)
            gate_or_up(0, 0, 0, 0)
            gate_or_up(0, 0, 1, 0)
            transpose_normed(NS, t_bank[NS], "norm2", "xT2")
            gate_or_up(1, 1, 0, 0)
            transpose_normed(NS + 1, t_bank[NS + 1], "norm2", "xT2")
            gate_or_up(1, 1, 1, 0)
            hold("x1_made", NT)
            logits_back(0)
            hold("xlo2", NT)
            logits_transposed(1)
            gate_or_up(0, 0, 0, 1).then_inc(s["gate_mm"], 1)
            logits_back(1)
            gate_or_up(0, 0, 1, 1).then_inc(s["up_mm"], 1)
            gate_or_up(1, 1, 0, 1).then_inc(s["gate_mm"], 1)
            gate_or_up(1, 1, 1, 1).then_inc(s["up_mm"], 1)
            hold("shared_g_made", 1)
            for tt in range(NT):
                last = mm(bank[4][:, tt * P:(tt + 1) * P], shared_g[:, tt:tt + 1].to_broadcast([P, P]), ident,
                          start=True, stop=True)
            last.then_inc(s["weight_mm"], 1)
            hold("route_made", 1)
            for tt in range(NT):
                last = nc.tensor.transpose(bank[7][0:E, tt * P:(tt + 1) * P], route[:, tt, :], ident)
            last.then_inc(s["routeT_made"], 1)
            gate_up(2, 2)
            hold("routeT_lo", 1)
            weight(1, 1, free=False)
            gate(3, 3)
            hold("routeT_full_made", 1)
            down(0, 0, first=True)
            weight(2, 2)
            up(3, 3)
            down(1, 1)
            down(2, 2)
            gate_up(RING, RING)
            down(RING - 1, RING - 1)
            with pe.Fori(1, (NP - 1) // RING - 1) as u:
                for j in range(1, RING + 1):
                    gate_up(j, u * RING + j)
                    down(j - 1, u * RING + j - 1)
            for q in range(NP - RING, NP - 1):
                gate_up(q, q)
                down(q - 1, q - 1)

            def back(b):
                hold("outT_copied", NC * (b + 1))
                for tt in range(b * NS, (b + 1) * NS):
                    for c in range(NC):
                        last = nc.tensor.transpose(bank[tt][:, c * P:(c + 1) * P], outT[:, c, tt * P:(tt + 1) * P],
                                                   ident)
                    last.then_inc(s["outT_t"], 1)

            q = NP - 1
            hold("w_lo", q + 1)
            hold("silu_made", q - 1)
            hold("gu_made", q - 1)
            for b in range(B):
                for k, (banks, made) in enumerate(((tail_gate_bank, "tail_gate"), (tail_up_bank, "tail_up"))):
                    parts_of(bank[banks[b]],
                             lambda c: ffn_hi[q % RING][:, (2 * c + k) * P:(2 * c + k + 1) * P],
                             lambda c: ffn_lo[q % RING][:, (2 * c + k) * P:(2 * c + k + 1) * P],
                             b).then_inc(s[made], 1)
            down(q - 1, q - 1)
            for b in range(B):
                hold("tail_ready", b + 1)
                if b:
                    hold("outT_copied", NC)
                down_parts(q % RING, slice(b * S, (b + 1) * S), last_pair=True).then_inc(s["tail_down"], 1)
            for b in range(B):
                back(b)


def kernel(x, ctx_512, g_xattn, g_ffn, L0_xattn_Wq, L0_xattn_w_kc_q, L0_xattn_w_kc_kv, L0_xattn_W_qr, L0_xattn_W_kr,
           L0_xattn_Wo, L0_ffn_gate_w, L0_ffn_gu_w, L0_ffn_dp_w, L0_ffn_sh_gate_w, L0_ffn_sh_up_w, L0_ffn_sh_down_w,
           L0_ffn_sh_gate1_w):
    import numpy as np
    import concourse.bacc as bacc
    from concourse.bass_utils import run_bass_kernel_spmd

    (x, ctx_512, g_xattn, g_ffn, Wq, kcq, kckv, Wqr, Wkr, Wo, gate, gu, dp, shg, shu, shd, shg1) = [
        np.asarray(a) for a in (x, ctx_512, g_xattn, g_ffn, L0_xattn_Wq, L0_xattn_w_kc_q, L0_xattn_w_kc_kv,
                                L0_xattn_W_qr, L0_xattn_W_kr, L0_xattn_Wo, L0_ffn_gate_w, L0_ffn_gu_w, L0_ffn_dp_w,
                                L0_ffn_sh_gate_w, L0_ffn_sh_up_w, L0_ffn_sh_down_w, L0_ffn_sh_gate1_w)]
    f32 = np.float32

    freq = f32(1.0) / f32(10000.0) ** (np.arange(0, DC, 2, dtype=f32) / f32(DC))
    angle = np.arange(L, dtype=f32)[:, None] * freq[None, :]
    cos = np.repeat(np.cos(angle), 2, axis=-1)
    sin = np.repeat(np.sin(angle), 2, axis=-1)
    sin = np.concatenate([-sin[:, :DC // 2], sin[:, DC // 2:]], axis=-1)
    rows = lambda a: a.reshape(NL, P, DC).transpose(1, 0, 2).reshape(P, NL * DC)
    consts = np.concatenate([np.eye(P, dtype=f32), rows(cos), rows(sin),
                             np.concatenate([np.eye(E, dtype=f32)] * 2)], axis=1).astype(f32)

    x_in = x.reshape(NT, P, DIM).transpose(1, 0, 2)
    ctx_in = ctx_512.reshape(B, NL, P, DC).transpose(2, 0, 1, 3)
    gains = np.broadcast_to(np.concatenate([g_xattn, g_ffn])[None, :], (P, 2))
    fq = np.concatenate([Wqr, kcq.transpose(0, 2, 1)], axis=2)
    fq = fq.reshape(HP, 2, 2, QH, R + HK).transpose(0, 3, 1, 2, 4).reshape(HP, QH, W1COLS)
    by_pair = lambda a: a.reshape(HP, 2, HK, -1).transpose(0, 2, 1, 3).reshape(HP, HK, -1)
    fa = np.concatenate([Wkr.transpose(0, 2, 1).reshape(HP, P, DC), by_pair(Wq.reshape(H, HK, DIM))], axis=2)
    fb = by_pair(np.concatenate([kckv, Wo.T.reshape(H, HK, DIM)], axis=2))
    by_chunk = lambda a: a.T.reshape(NC, P, -1).transpose(1, 0, 2)
    gate_in = by_chunk(gate)
    g1_in = np.broadcast_to(shg1, (P, DIM))
    gu_sh = np.zeros((2, 2, EI, DIM), f32)
    gu_sh[0, 0], gu_sh[1, 0] = shg, shu
    gu_all = gu.reshape(EP, 2, 2, EI, DIM).transpose(0, 2, 1, 3, 4)
    gu_all = np.concatenate([gu_sh[None], gu_all]).reshape(NP, 2, P, NC, P).transpose(0, 4, 3, 1, 2)
    dp_sh = np.zeros((2, EI, DIM), f32)
    dp_sh[0] = shd.T
    dp_all = np.concatenate([dp_sh[None], dp.transpose(0, 2, 1).reshape(EP, 2, EI, DIM)]).reshape(NP, P, DIM)
    experts = np.concatenate([gu_all.reshape(NP, P, GU), dp_all], axis=2)

    arrays = {"x": x_in, "ctx": ctx_in, "consts": consts, "gains": gains,
              "w_fold_r": fq, "w_fold_a": fa, "w_fold_b": fb,
              "gate_w": gate_in, "shared_gate1": g1_in, "w_experts": experts}
    nc = bacc.Bacc("TRN2", target_bir_lowering=False, num_devices=1)
    ins, args = {}, []
    for name, a in arrays.items():
        a = np.ascontiguousarray(a)
        ins[f"in_{name}"] = a
        args.append(nc.dram_tensor(f"in_{name}", a.shape, mybir.dt.from_np(a.dtype), kind="ExternalInput").ap())
    out = nc.dram_tensor("result", (TOK, DIM), F32, kind="ExternalOutput").ap()
    routed = nc.dram_tensor("routed", (E, TOK), F32, kind="Internal").ap()
    gated_cross_attention_moe(nc, *args, routed, out.rearrange("(t p) c -> p t c", p=P))
    r = run_bass_kernel_spmd(nc, [ins], core_ids=[0])
    return r.results[0]["result"].reshape(B, S, DIM)
```
